# Optimizing a Trainium2 kernel written in Bass

```python
import numpy as np
import jax
import jax.numpy as jnp

def _softmax(x, axis=-1):
    return jax.nn.softmax(x, axis=axis)

def _gelu(x):
    return jax.nn.gelu(x, approximate=True)

def _silu(x):
    return jax.nn.silu(x)

def _sigmoid(x):
    return jax.nn.sigmoid(x)

def _layernorm(x, axis=-1, eps=1e-05):
    m = jnp.mean(x, axis=axis, keepdims=True)
    v = jnp.var(x, axis=axis, keepdims=True)
    return (x - m) / jnp.sqrt(v + eps)

def _scatter_add(tgt, idx, src, axis=0):
    return tgt.at[idx].add(src)

def _segment_sum(src, seg, n):
    return jax.ops.segment_sum(src, seg, n)
kernel_name = 'mk_dlrm_tower_d1_rec_r8_bd1ec0'

def setup_inputs(seed: int=0):
    np.random.seed(seed)
    _w = jnp.asarray

    def _rec_inputs():
        import jax
        import jax.numpy as jnp
        _tk = jax.random.key(seed)
        dense_ctx = jax.random.normal(jax.random.fold_in(_tk, 190), (512, 16), jnp.float32)
        ids = jnp.stack([jax.random.randint(jax.random.fold_in(_tk, 200 + f), (512,), 0, v, jnp.int32) for f, v in enumerate([125000, 1000, 125000, 12500, 12500, 1250, 1000, 1000, 12500, 1250, 125000, 1250, 125000, 1250, 1250, 1000, 125000, 12500, 12500, 125000, 1000, 125000, 1250, 1250, 1250, 125000, 125000, 12500, 1000, 1000, 1250, 125000, 1250, 1000, 1250, 12500, 1000, 12500, 12500])], axis=1)
        tbl_0 = 0.05 * jax.random.normal(jax.random.fold_in(_tk, 500 + 0), (125000, 16), jnp.float32)
        tbl_1 = 0.05 * jax.random.normal(jax.random.fold_in(_tk, 500 + 1), (1000, 16), jnp.float32)
        tbl_2 = 0.05 * jax.random.normal(jax.random.fold_in(_tk, 500 + 2), (125000, 16), jnp.float32)
        tbl_3 = 0.05 * jax.random.normal(jax.random.fold_in(_tk, 500 + 3), (12500, 16), jnp.float32)
        tbl_4 = 0.05 * jax.random.normal(jax.random.fold_in(_tk, 500 + 4), (12500, 16), jnp.float32)
        tbl_5 = 0.05 * jax.random.normal(jax.random.fold_in(_tk, 500 + 5), (1250, 16), jnp.float32)
        tbl_6 = 0.05 * jax.random.normal(jax.random.fold_in(_tk, 500 + 6), (1000, 16), jnp.float32)
        tbl_7 = 0.05 * jax.random.normal(jax.random.fold_in(_tk, 500 + 7), (1000, 16), jnp.float32)
        tbl_8 = 0.05 * jax.random.normal(jax.random.fold_in(_tk, 500 + 8), (12500, 16), jnp.float32)
        tbl_9 = 0.05 * jax.random.normal(jax.random.fold_in(_tk, 500 + 9), (1250, 16), jnp.float32)
        tbl_10 = 0.05 * jax.random.normal(jax.random.fold_in(_tk, 500 + 10), (125000, 16), jnp.float32)
        tbl_11 = 0.05 * jax.random.normal(jax.random.fold_in(_tk, 500 + 11), (1250, 16), jnp.float32)
        tbl_12 = 0.05 * jax.random.normal(jax.random.fold_in(_tk, 500 + 12), (125000, 16), jnp.float32)
        tbl_13 = 0.05 * jax.random.normal(jax.random.fold_in(_tk, 500 + 13), (1250, 16), jnp.float32)
        tbl_14 = 0.05 * jax.random.normal(jax.random.fold_in(_tk, 500 + 14), (1250, 16), jnp.float32)
        tbl_15 = 0.05 * jax.random.normal(jax.random.fold_in(_tk, 500 + 15), (1000, 16), jnp.float32)
        tbl_16 = 0.05 * jax.random.normal(jax.random.fold_in(_tk, 500 + 16), (125000, 16), jnp.float32)
        tbl_17 = 0.05 * jax.random.normal(jax.random.fold_in(_tk, 500 + 17), (12500, 16), jnp.float32)
        tbl_18 = 0.05 * jax.random.normal(jax.random.fold_in(_tk, 500 + 18), (12500, 16), jnp.float32)
        tbl_19 = 0.05 * jax.random.normal(jax.random.fold_in(_tk, 500 + 19), (125000, 16), jnp.float32)
        tbl_20 = 0.05 * jax.random.normal(jax.random.fold_in(_tk, 500 + 20), (1000, 16), jnp.float32)
        tbl_21 = 0.05 * jax.random.normal(jax.random.fold_in(_tk, 500 + 21), (125000, 16), jnp.float32)
        tbl_22 = 0.05 * jax.random.normal(jax.random.fold_in(_tk, 500 + 22), (1250, 16), jnp.float32)
        tbl_23 = 0.05 * jax.random.normal(jax.random.fold_in(_tk, 500 + 23), (1250, 16), jnp.float32)
        tbl_24 = 0.05 * jax.random.normal(jax.random.fold_in(_tk, 500 + 24), (1250, 16), jnp.float32)
        tbl_25 = 0.05 * jax.random.normal(jax.random.fold_in(_tk, 500 + 25), (125000, 16), jnp.float32)
        tbl_26 = 0.05 * jax.random.normal(jax.random.fold_in(_tk, 500 + 26), (125000, 16), jnp.float32)
        tbl_27 = 0.05 * jax.random.normal(jax.random.fold_in(_tk, 500 + 27), (12500, 16), jnp.float32)
        tbl_28 = 0.05 * jax.random.normal(jax.random.fold_in(_tk, 500 + 28), (1000, 16), jnp.float32)
        tbl_29 = 0.05 * jax.random.normal(jax.random.fold_in(_tk, 500 + 29), (1000, 16), jnp.float32)
        tbl_30 = 0.05 * jax.random.normal(jax.random.fold_in(_tk, 500 + 30), (1250, 16), jnp.float32)
        tbl_31 = 0.05 * jax.random.normal(jax.random.fold_in(_tk, 500 + 31), (125000, 16), jnp.float32)
        tbl_32 = 0.05 * jax.random.normal(jax.random.fold_in(_tk, 500 + 32), (1250, 16), jnp.float32)
        tbl_33 = 0.05 * jax.random.normal(jax.random.fold_in(_tk, 500 + 33), (1000, 16), jnp.float32)
        tbl_34 = 0.05 * jax.random.normal(jax.random.fold_in(_tk, 500 + 34), (1250, 16), jnp.float32)
        tbl_35 = 0.05 * jax.random.normal(jax.random.fold_in(_tk, 500 + 35), (12500, 16), jnp.float32)
        tbl_36 = 0.05 * jax.random.normal(jax.random.fold_in(_tk, 500 + 36), (1000, 16), jnp.float32)
        tbl_37 = 0.05 * jax.random.normal(jax.random.fold_in(_tk, 500 + 37), (12500, 16), jnp.float32)
        tbl_38 = 0.05 * jax.random.normal(jax.random.fold_in(_tk, 500 + 38), (12500, 16), jnp.float32)
        _rk = jax.random.fold_in(_tk, 7)
        W_top1 = 0.0606339 * jax.random.normal(jax.random.fold_in(_tk, 801), (272, 512), jnp.float32)
        W_top2 = 0.0441942 * jax.random.normal(jax.random.fold_in(_tk, 802), (512, 256), jnp.float32)
        W_top3 = 0.0625 * jax.random.normal(jax.random.fold_in(_tk, 803), (256, 1), jnp.float32)
        b_top1 = jnp.zeros((512,), jnp.float32)
        b_top2 = jnp.zeros((256,), jnp.float32)
        return (dense_ctx, ids, tbl_0, tbl_1, tbl_2, tbl_3, tbl_4, tbl_5, tbl_6, tbl_7, tbl_8, tbl_9, tbl_10, tbl_11, tbl_12, tbl_13, tbl_14, tbl_15, tbl_16, tbl_17, tbl_18, tbl_19, tbl_20, tbl_21, tbl_22, tbl_23, tbl_24, tbl_25, tbl_26, tbl_27, tbl_28, tbl_29, tbl_30, tbl_31, tbl_32, tbl_33, tbl_34, tbl_35, tbl_36, tbl_37, tbl_38, W_top1, b_top1, W_top2, b_top2, W_top3)
    dense_ctx, ids, tbl_0, tbl_1, tbl_2, tbl_3, tbl_4, tbl_5, tbl_6, tbl_7, tbl_8, tbl_9, tbl_10, tbl_11, tbl_12, tbl_13, tbl_14, tbl_15, tbl_16, tbl_17, tbl_18, tbl_19, tbl_20, tbl_21, tbl_22, tbl_23, tbl_24, tbl_25, tbl_26, tbl_27, tbl_28, tbl_29, tbl_30, tbl_31, tbl_32, tbl_33, tbl_34, tbl_35, tbl_36, tbl_37, tbl_38, W_top1, b_top1, W_top2, b_top2, W_top3 = _rec_inputs()

    def _L0_rec_setup():
        import jax, jax.numpy as jnp
        import numpy as np
        B, F0, D = (256, 39, 16)
        LAYER_SIZES = [128, 128, 128]
        key = jax.random.key(seed)
        ks = jax.random.split(key, 1 + 2 * len(LAYER_SIZES))
        inputs = jax.random.normal(ks[0], (B, F0, D), dtype=jnp.float32)
        out = {'inputs': inputs}
        field_nums = [F0]
        for i, size in enumerate(LAYER_SIZES):
            fk = field_nums[-1]
            fan_in = F0 * fk
            scale = np.sqrt(2.0 / (fan_in + size)).astype(np.float32)
            out[f'w{i}'] = jax.random.normal(ks[1 + 2 * i], (F0, fk, size), dtype=jnp.float32) * scale
            out[f'b{i}'] = jnp.zeros((size,), dtype=jnp.float32)
            field_nums.append(size // 2)
        return out
    _L0_rec_all = _L0_rec_setup()
    _L0_rec_in = {k: v for k, v in _L0_rec_all.items() if k in ('w0', 'w1', 'w2', 'b0', 'b1', 'b2')}
    del _L0_rec_all
    return {'dense_ctx': dense_ctx, 'ids': ids, 'tbl_0': tbl_0, 'tbl_1': tbl_1, 'tbl_2': tbl_2, 'tbl_3': tbl_3, 'tbl_4': tbl_4, 'tbl_5': tbl_5, 'tbl_6': tbl_6, 'tbl_7': tbl_7, 'tbl_8': tbl_8, 'tbl_9': tbl_9, 'tbl_10': tbl_10, 'tbl_11': tbl_11, 'tbl_12': tbl_12, 'tbl_13': tbl_13, 'tbl_14': tbl_14, 'tbl_15': tbl_15, 'tbl_16': tbl_16, 'tbl_17': tbl_17, 'tbl_18': tbl_18, 'tbl_19': tbl_19, 'tbl_20': tbl_20, 'tbl_21': tbl_21, 'tbl_22': tbl_22, 'tbl_23': tbl_23, 'tbl_24': tbl_24, 'tbl_25': tbl_25, 'tbl_26': tbl_26, 'tbl_27': tbl_27, 'tbl_28': tbl_28, 'tbl_29': tbl_29, 'tbl_30': tbl_30, 'tbl_31': tbl_31, 'tbl_32': tbl_32, 'tbl_33': tbl_33, 'tbl_34': tbl_34, 'tbl_35': tbl_35, 'tbl_36': tbl_36, 'tbl_37': tbl_37, 'tbl_38': tbl_38, 'W_top1': W_top1, 'b_top1': b_top1, 'W_top2': W_top2, 'b_top2': b_top2, 'W_top3': W_top3, 'L0_rec_w0': _L0_rec_in['w0'], 'L0_rec_w1': _L0_rec_in['w1'], 'L0_rec_w2': _L0_rec_in['w2'], 'L0_rec_b0': _L0_rec_in['b0'], 'L0_rec_b1': _L0_rec_in['b1'], 'L0_rec_b2': _L0_rec_in['b2']}

def reference(dense_ctx, ids, tbl_0, tbl_1, tbl_2, tbl_3, tbl_4, tbl_5, tbl_6, tbl_7, tbl_8, tbl_9, tbl_10, tbl_11, tbl_12, tbl_13, tbl_14, tbl_15, tbl_16, tbl_17, tbl_18, tbl_19, tbl_20, tbl_21, tbl_22, tbl_23, tbl_24, tbl_25, tbl_26, tbl_27, tbl_28, tbl_29, tbl_30, tbl_31, tbl_32, tbl_33, tbl_34, tbl_35, tbl_36, tbl_37, tbl_38, W_top1, b_top1, W_top2, b_top2, W_top3, L0_rec_w0, L0_rec_w1, L0_rec_w2, L0_rec_b0, L0_rec_b1, L0_rec_b2):
    import jax
    import jax.numpy as jnp

    def _L0_rec_ref(inputs, w0, w1, w2, b0, b1, b2):
        import jax, jax.numpy as jnp
        import numpy as np
        B, F0, D = (256, 39, 16)
        LAYER_SIZES = [128, 128, 128]
        x0 = inputs
        xk = inputs
        params = [(w0, b0), (w1, b1), (w2, b2)]
        n_layers = len(params)
        direct = []
        for idx, (W, b) in enumerate(params):
            z = jnp.einsum('bhd,bkd,hks->bsd', x0, xk, W) + b[None, :, None]
            z = jax.nn.relu(z)
            if idx != n_layers - 1:
                half = z.shape[1] // 2
                xk = z[:, :half, :]
                direct.append(z[:, half:, :])
            else:
                direct.append(z)
        logit = jnp.sum(jnp.concatenate(direct, axis=1), axis=-1)
        return logit
    e = jnp.stack([tbl_0[ids[:, 0]], tbl_1[ids[:, 1]], tbl_2[ids[:, 2]], tbl_3[ids[:, 3]], tbl_4[ids[:, 4]], tbl_5[ids[:, 5]], tbl_6[ids[:, 6]], tbl_7[ids[:, 7]], tbl_8[ids[:, 8]], tbl_9[ids[:, 9]], tbl_10[ids[:, 10]], tbl_11[ids[:, 11]], tbl_12[ids[:, 12]], tbl_13[ids[:, 13]], tbl_14[ids[:, 14]], tbl_15[ids[:, 15]], tbl_16[ids[:, 16]], tbl_17[ids[:, 17]], tbl_18[ids[:, 18]], tbl_19[ids[:, 19]], tbl_20[ids[:, 20]], tbl_21[ids[:, 21]], tbl_22[ids[:, 22]], tbl_23[ids[:, 23]], tbl_24[ids[:, 24]], tbl_25[ids[:, 25]], tbl_26[ids[:, 26]], tbl_27[ids[:, 27]], tbl_28[ids[:, 28]], tbl_29[ids[:, 29]], tbl_30[ids[:, 30]], tbl_31[ids[:, 31]], tbl_32[ids[:, 32]], tbl_33[ids[:, 33]], tbl_34[ids[:, 34]], tbl_35[ids[:, 35]], tbl_36[ids[:, 36]], tbl_37[ids[:, 37]], tbl_38[ids[:, 38]]], axis=1)
    z = _L0_rec_ref(e, L0_rec_w0, L0_rec_w1, L0_rec_w2, L0_rec_b0, L0_rec_b1, L0_rec_b2)
    z = z.reshape(z.shape[0], -1)
    h = jnp.concatenate([z, dense_ctx], axis=1)
    h = jnp.maximum(h @ W_top1 + b_top1, 0.0)
    h = jnp.maximum(h @ W_top2 + b_top2, 0.0)
    y = h @ W_top3
    return y

_drawn_inputs = setup_inputs


def setup_inputs(seed=0):
    import zlib

    import numpy as np

    out = dict(_drawn_inputs(seed))
    spreads = {'b_top1': (0.0, 2.0),
     'b_top2': (0.0, 2.0),
     'L0_rec_b0': (0.0, 0.36),
     'L0_rec_b1': (0.0, 0.508),
     'L0_rec_b2': (0.0, 0.8)}
    factors = {'tbl_0': 8.0,
     'tbl_1': 8.0,
     'tbl_2': 8.0,
     'tbl_3': 8.0,
     'tbl_4': 8.0,
     'tbl_5': 8.0,
     'tbl_6': 8.0,
     'tbl_7': 8.0,
     'tbl_8': 8.0,
     'tbl_9': 8.0,
     'tbl_10': 8.0,
     'tbl_11': 8.0,
     'tbl_12': 8.0,
     'tbl_13': 8.0,
     'tbl_14': 8.0,
     'tbl_15': 8.0,
     'tbl_16': 8.0,
     'tbl_17': 8.0,
     'tbl_18': 8.0,
     'tbl_19': 8.0,
     'tbl_20': 8.0,
     'tbl_21': 8.0,
     'tbl_22': 8.0,
     'tbl_23': 8.0,
     'tbl_24': 8.0,
     'tbl_25': 8.0,
     'tbl_26': 8.0,
     'tbl_27': 8.0,
     'tbl_28': 8.0,
     'tbl_29': 8.0,
     'tbl_30': 8.0,
     'tbl_31': 8.0,
     'tbl_32': 8.0,
     'tbl_33': 8.0,
     'tbl_34': 8.0,
     'tbl_35': 8.0,
     'tbl_36': 8.0,
     'tbl_37': 8.0,
     'tbl_38': 8.0,
     'L0_rec_w0': 8.0,
     'L0_rec_w1': 6.277,
     'L0_rec_w2': 4.672,
     'dense_ctx': 8.0}
    for name, (base, spread) in spreads.items():
        noise = np.random.default_rng([zlib.crc32(name.encode()), seed]).standard_normal(out[name].shape)
        drawn = base * np.exp(spread * noise) if base else spread * noise
        out[name] = jnp.asarray(drawn.astype(out[name].dtype))
    for name, factor in factors.items():
        out[name] = (out[name] * factor).astype(out[name].dtype)
    return out
```

```python
from contextlib import ExitStack

import numpy as np

import concourse.bass as bass
from concourse import mybir

F32 = mybir.dt.float32
BF16 = mybir.dt.bfloat16
I32 = mybir.dt.int32
ALU = mybir.AluOpType
ACT = mybir.ActivationFunctionType
AX_X = mybir.AxisListType.X

BATCH = 512
FIELDS = 39
DIM = 16
MAPS = 128
HALF = MAPS // 2
DENSE = 16
HID1, HID2 = 512, 256
P = 128

CHUNK_ROWS = 32
COLS = CHUNK_ROWS * DIM
CHUNKS = BATCH // CHUNK_ROWS

REP = 3
RF = REP * FIELDS
SLOTS = -(-CHUNK_ROWS // REP)
SLOT_ROWS = [min(REP, CHUNK_ROWS - REP * i) for i in range(SLOTS)]

SHIFTS = (FIELDS + 1) // 2
L0_TILES = -(-SHIFTS // REP)
L0_ROWS = [min(REP, SHIFTS - REP * j) * FIELDS for j in range(L0_TILES)]
L12_TILES = -(-FIELDS // 2)
L12_ROWS = [min(2, FIELDS - 2 * t) * HALF for t in range(L12_TILES)]

SPREADS = L0_TILES + L12_TILES
PRODUCTS = L0_TILES + 2 * L12_TILES
PROLOGUE = L0_TILES + L12_TILES
SPREAD_BANKS = 3
PRODUCT_SLOTS = 16
REUSE = min(PRODUCT_SLOTS, PRODUCTS - PRODUCT_SLOTS * ((PRODUCTS - 1) // PRODUCT_SLOTS))
LEAD = 5
SPLIT_STEPS = 6
assert SPREADS % SPREAD_BANKS == 0


def interaction_tower(nc, tables, ids, bases, x_select, shift_select, field_select,
                      w0_upper, w0_lower, w1, w2, b0, b1, b2,
                      dense_t, w_top1, b_top1, w_top2, b_top2, w_top3, out):
    ctx = ExitStack()
    with ctx:
        def sb(name, shape, dt=F32):
            return ctx.enter_context(nc.sbuf_tensor(name, shape, dt))

        def bank(name):
            return ctx.enter_context(nc.psum_tensor(name, [P, COLS], F32))

        def sem(name):
            return ctx.enter_context(nc.semaphore(name))

        ids_sb = sb("ids_sb", [RF, CHUNKS * SLOTS], I32)
        bases_sb = sb("bases_sb", [RF, CHUNKS * SLOTS], I32)
        rows_sb = sb("rows_sb", [RF, CHUNKS * SLOTS], I32)
        x_sel = sb("x_sel", [RF, REP, RF])
        shift_sel = sb("shift_sel", [RF, L0_TILES, RF], BF16)
        field_sel = sb("field_sel", [RF, L12_TILES, P], BF16)
        w0u_sb = sb("w0u_sb", [RF, L0_TILES, MAPS])
        w0l_sb = sb("w0l_sb", [RF, L0_TILES, MAPS])
        w0_sb = sb("w0_sb", [RF, L0_TILES, MAPS])
        w1_sb = sb("w1_sb", [P, L12_TILES, MAPS])
        w2_sb = sb("w2_sb", [P, L12_TILES, MAPS])
        bias_sb = sb("bias_sb", [P, 3])
        wt1_sb = sb("wt1_sb", [P, 2, HID1])
        wt1d_sb = sb("wt1d_sb", [DENSE, HID1])
        bt1_sb = sb("bt1_sb", [P, HID1 // P])
        wt2_sb = sb("wt2_sb", [P, HID1 // P, HID2])
        bt2_sb = sb("bt2_sb", [P, HID2 // P])
        wt3_sb = sb("wt3_sb", [P, HID2 // P])
        dense_sb = sb("dense_sb", [DENSE, BATCH])

        rows_now = sb("rows_now", [RF, SLOTS], I32)
        gathered = sb("gathered", [RF, SLOTS * DIM])
        x_rep = sb("x_rep", [RF, COLS])
        x_hi = sb("x_hi", [RF, COLS], BF16)
        x_rest = sb("x_rest", [RF, COLS])
        x_mid = sb("x_mid", [RF, COLS], BF16)
        parts_a = sb("parts_a", [RF, COLS], BF16)
        parts_b = sb("parts_b", [RF, COLS], BF16)
        spread_sb = sb("spread_sb", [P, L12_TILES, COLS])
        products = sb("products", [P, PRODUCT_SLOTS, COLS])
        x1 = sb("x1", [P, COLS])
        x2 = sb("x2", [P, COLS])
        direct0 = sb("direct0", [P, COLS])
        direct1 = sb("direct1", [P, COLS])
        direct2 = sb("direct2", [P, COLS])
        feats = sb("feats", [P, 2, BATCH])
        hid1 = sb("hid1", [P, HID1 // P, BATCH])
        hid2 = sb("hid2", [P, HID2 // P, BATCH])
        y_sb = sb("y_sb", [1, BATCH])

        x_bank = bank("x_bank")
        spread_banks = [bank(f"spread_bank{n}") for n in range(SPREAD_BANKS)]
        z0, z1, z2 = bank("z0"), bank("z1"), bank("z2")
        y_bank = bank("y_bank")
        tower_banks = [z0, z1, z2, x_bank, spread_banks[0], spread_banks[1]]

        ids_in = sem("ids_in")
        consts_in = sem("consts_in")
        w0_in = sem("w0_in")
        w12_in = sem("w12_in")
        tower_in = sem("tower_in")
        pool_waits = sem("pool_waits")
        rows_known = sem("rows_known")
        w0_ready = sem("w0_ready")
        rows_copied = sem("rows_copied")
        gathers_done = sem("gathers_done")
        x_selected = sem("x_selected")
        x_copied = sem("x_copied")
        split_steps = sem("split_steps")
        parts_a_ready = sem("parts_a_ready")
        parts_b_ready = sem("parts_b_ready")
        spreads_done = sem("spreads_done")
        spreads_copied = sem("spreads_copied")
        products_ready = sem("products_ready")
        products_used = sem("products_used")
        z0_ready = sem("z0_ready")
        z1_ready = sem("z1_ready")
        z2_ready = sem("z2_ready")
        z0_read = sem("z0_read")
        z1_read = sem("z1_read")
        z2_read = sem("z2_read")
        direct0_summed = sem("direct0_summed")
        direct1_summed = sem("direct1_summed")
        direct2_summed = sem("direct2_summed")
        tower_mm = sem("tower_mm")
        tower_act = sem("tower_act")
        stored = sem("stored")

        block = ctx.enter_context(nc.Block())

        def before_l0(c):
            return PRODUCTS * (c - 1) + PROLOGUE

        def before_l1(c):
            return PRODUCTS * c + L0_TILES

        def before_l2(c):
            return before_l0(c + 1) + L0_TILES

        L0_AT, L2_AT, L1_AT = 0, L0_TILES, L0_TILES + L12_TILES
        PROLOGUE_L0_AT = PRODUCTS - PROLOGUE

        def slot(place):
            return products[:, place % PRODUCT_SLOTS, :]

        @block.sync
        def _(sp):
            sp.dma_start(ids_sb[:, :], ids).then_inc(ids_in, 16)
            sp.dma_start(bases_sb[:, :], bases).then_inc(ids_in, 16)
            sp.dma_start(x_sel[:, :, :], x_select).then_inc(consts_in, 16)
            sp.dma_start(shift_sel[:, :, :], shift_select).then_inc(consts_in, 16)
            sp.dma_start(field_sel[:, :, :], field_select).then_inc(consts_in, 16)
            sp.dma_start(bias_sb[:, 0:1], b0).then_inc(consts_in, 16)
            sp.dma_start(bias_sb[:, 1:2], b1).then_inc(consts_in, 16)
            sp.dma_start(bias_sb[:, 2:3], b2).then_inc(consts_in, 16)
            sp.dma_start(w0u_sb[:, :, :], w0_upper).then_inc(w0_in, 16)
            sp.dma_start(w0l_sb[:, :, :], w0_lower).then_inc(w0_in, 16)
            whole = (L12_TILES - 1) * P
            for w_sb, w in ((w1_sb, w1), (w2_sb, w2)):
                sp.dma_start(w_sb[:, 0:L12_TILES - 1, :],
                             w[0:whole, :].rearrange("(t p) s -> p t s", p=P)).then_inc(w12_in, 16)
                sp.dma_start(w_sb[0:HALF, L12_TILES - 1, :], w[whole:whole + HALF, :]).then_inc(w12_in, 16)
            sp.dma_start(wt1_sb[:, :, :], w_top1[0:2 * P, :].rearrange("(a p) m -> p a m", p=P)).then_inc(tower_in, 16)
            sp.dma_start(wt1d_sb[:, :], w_top1[2 * P:2 * P + DENSE, :]).then_inc(tower_in, 16)
            sp.dma_start(wt2_sb[:, :, :], w_top2.rearrange("(a p) m -> p a m", p=P)).then_inc(tower_in, 16)
            sp.dma_start(bt1_sb[:, :], b_top1).then_inc(tower_in, 16)
            sp.dma_start(bt2_sb[:, :], b_top2).then_inc(tower_in, 16)
            sp.dma_start(wt3_sb[:, :], w_top3).then_inc(tower_in, 16)
            sp.dma_start(dense_sb[:, :], dense_t).then_inc(tower_in, 16)
            sp.wait_ge(tower_act, HID1 // P + HID2 // P + 1)
            sp.dma_start(out, y_sb[:, :]).then_inc(stored, 16)
            sp.wait_ge(stored, 16)

        @block.gpsimd
        def _(pool):
            def wait(semaphore, count):
                pool.wait_ge(semaphore, count)
                pool.sem_inc(pool_waits, 1)

            def gather(c):
                nc.gpsimd.tensor_copy(rows_now[:, :], rows_sb[:, bass.ds(c * SLOTS, SLOTS)]).then_inc(rows_copied, 1)
                wait(rows_copied, c + 1)
                for i in range(SLOTS):
                    n = SLOT_ROWS[i] * FIELDS
                    nc.gpsimd.indirect_dma_start(
                        out=gathered[0:n, i * DIM:(i + 1) * DIM], out_offset=None, in_=tables,
                        in_offset=bass.IndirectOffsetOnAxis(ap=rows_now[0:n, i:i + 1], axis=0),
                    ).then_inc(gathers_done, 16)

            def split(c):
                def link(ins, k):
                    ins.then_inc(split_steps, 1)
                    wait(split_steps, SPLIT_STEPS * c + k)

                wait(x_copied, c + 1)
                link(nc.gpsimd.tensor_copy(x_hi[:, :], x_rep[:, :]), 1)
                link(nc.gpsimd.tensor_tensor(x_rest[:, :], x_rep[:, :], x_hi[:, :], ALU.subtract), 2)
                link(nc.gpsimd.tensor_copy(x_mid[:, :], x_rest[:, :]), 3)
                link(nc.gpsimd.tensor_tensor(parts_a[:, :], x_rest[:, :], x_mid[:, :], ALU.subtract), 4)
                link(nc.gpsimd.tensor_copy(parts_a[0:2 * FIELDS, :], x_mid[0:2 * FIELDS, :]), 5)
                nc.gpsimd.tensor_copy(parts_a[0:FIELDS, :], x_hi[0:FIELDS, :]).then_inc(split_steps, 1)
                pool.wait_ge(split_steps, SPLIT_STEPS * (c + 1))
                pool.sem_inc(parts_a_ready, 1)

            def keep_parts():
                nc.gpsimd.tensor_copy(parts_b[:, :], parts_a[:, :]).then_inc(parts_b_ready, 1)

            wait(rows_known, 1)
            gather(0)
            split(0)
            keep_parts()
            wait(x_selected, 1)
            gather(1)
            wait(spreads_done, L0_TILES)
            wait(parts_b_ready, 1)
            split(1)
            wait(x_selected, 2)
            gather(2)

            def step(c, more, gathers):
                wait(spreads_done, SPREADS * (c + 1))
                keep_parts()
                if more:
                    wait(spreads_done, SPREADS * (c + 1) + L0_TILES)
                    wait(parts_b_ready, c + 2)
                    split(c + 2)
                if gathers:
                    wait(x_selected, c + 3)
                    gather(c + 3)

            with pool.Fori(0, CHUNKS - 3) as c:
                step(c, True, True)
            step(CHUNKS - 3, True, False)
            step(CHUNKS - 2, False, False)

        @block.scalar
        def _(act):
            def copy_x(c, products_before):
                act.wait_ge(x_selected, c + 1)
                if products_before is not None:
                    act.wait_ge(products_ready, products_before)
                nc.scalar.activation(x_rep[:, :], x_bank[0:RF, :], ACT.Copy).then_inc(x_copied, 1)

            def layer_out(z, z_ready, z_read, n, x_next, direct, bias_at, x_used, summed, summed_start=0):
                act.wait_ge(z_ready, n + 1)
                act.wait_ge(products_ready, x_used)
                bias = bias_sb[:, bias_at:bias_at + 1]
                nc.scalar.activation(x_next[0:HALF, :], z[0:HALF, :], ACT.Relu, bias=bias[0:HALF]).then_inc(z_read, 1)
                nc.scalar.activation(x_next[HALF:P, :], z[0:HALF, :], ACT.Relu, bias=bias[0:HALF]).then_inc(z_read, 1)
                if summed is not None:
                    act.wait_ge(summed, n + summed_start)
                nc.scalar.activation(direct[HALF:P, :], z[HALF:P, :], ACT.Relu, bias=bias[HALF:P]).then_inc(z_read, 1)

            def copy_spread(c, t, wait_l2):
                act.wait_ge(spreads_done, SPREADS * c + L0_TILES + t + 1)
                if wait_l2:
                    act.wait_ge(products_ready, before_l2(c - 1) + t + 1)
                n = L12_ROWS[t]
                bank_ = spread_banks[(L0_TILES + t) % SPREAD_BANKS]
                nc.scalar.activation(spread_sb[0:n, t, :], bank_[0:n, :], ACT.Copy).then_inc(spreads_copied, 1)

            act.sem_inc(z2_read, 1)
            act.wait_ge(consts_in, 6 * 16)
            copy_x(0, None)
            for t in range(L12_TILES):
                if t == LEAD - 1:
                    layer_out(z0, z0_ready, z0_read, 0, x1, direct0, 0, 1, None)
                copy_spread(0, t, False)
                if t == 14:
                    copy_x(1, L0_TILES)

            def layer2_out(c):
                act.wait_ge(z2_ready, c + 1)
                act.wait_ge(direct2_summed, c + 1)
                nc.scalar.activation(direct2[:, :], z2[:, :], ACT.Relu, bias=bias_sb[:, 2:3]).then_inc(z2_read, 1)

            def step(c, more):
                layer_out(z1, z1_ready, z1_read, c, x2, direct1, 1, before_l1(c), direct1_summed, 1)
                layer_out(z0, z0_ready, z0_read, c + 1, x1, direct0, 0, before_l0(c + 1), direct0_summed)
                if more:
                    copy_x(c + 2, before_l0(c + 1) + L0_TILES)
                for t in range(L12_TILES):
                    copy_spread(c + 1, t, True)
                    if t == LEAD + 1:
                        layer2_out(c)

            with act.Fori(0, CHUNKS - 2) as c:
                step(c, True)
            step(CHUNKS - 2, False)
            layer_out(z1, z1_ready, z1_read, CHUNKS - 1, x2, direct1, 1, before_l1(CHUNKS - 1), direct1_summed, 1)
            layer2_out(CHUNKS - 1)

            act.wait_ge(tower_in, 7 * 16)
            for m in range(HID1 // P):
                act.wait_ge(tower_mm, m + 1)
                nc.scalar.activation(hid1[:, m, :], tower_banks[m][:, :], ACT.Relu,
                                     bias=bt1_sb[:, m:m + 1]).then_inc(tower_act, 1)
            for m in range(HID2 // P):
                act.wait_ge(tower_mm, HID1 // P + m + 1)
                nc.scalar.activation(hid2[:, m, :], tower_banks[HID1 // P + m][:, :], ACT.Relu,
                                     bias=bt2_sb[:, m:m + 1]).then_inc(tower_act, 1)
            act.wait_ge(tower_mm, HID1 // P + HID2 // P + 1)
            nc.scalar.activation(y_sb[:, :], y_bank[0:1, :], ACT.Copy).then_inc(tower_act, 1)

        @block.vector
        def _(dve):
            dve.sem_inc(direct1_summed, 1)
            dve.sem_inc(direct2_summed, 1)
            dve.wait_ge(ids_in, 2 * 16)
            nc.vector.tensor_tensor(rows_sb[:, :], ids_sb[:, :], bases_sb[:, :], ALU.add).then_inc(rows_known, 1)
            dve.wait_ge(w0_in, 2 * 16)
            nc.vector.tensor_tensor(w0_sb[:, :, :], w0u_sb[:, :, :], w0l_sb[:, :, :], ALU.add).then_inc(w0_ready, 1)

            def wait_slot(made):
                need = made + 1 - REUSE
                if not isinstance(need, int) or need > 0:
                    dve.wait_ge(products_used, need)

            def l0_products(c, made, place):
                dve.wait_ge(x_copied, c + 1)
                for j in range(L0_TILES):
                    n = L0_ROWS[j]
                    dve.wait_ge(spreads_done, SPREADS * c + j + 1)
                    wait_slot(made + j)
                    nc.vector.tensor_tensor(slot(place + j)[0:n, :], spread_banks[j % SPREAD_BANKS][0:n, :],
                                            x_rep[0:n, :], ALU.mult).then_inc(products_ready, 1)

            def l12_product(t, x, made, place):
                n = L12_ROWS[t]
                wait_slot(made + t)
                nc.vector.tensor_tensor(slot(place + t)[0:n, :], spread_sb[0:n, t, :], x[0:n, :],
                                        ALU.mult).then_inc(products_ready, 1)

            def l1_product(c, t, made, place):
                dve.wait_ge(spreads_copied, L12_TILES * c + t + 1)
                l12_product(t, x1, made, place)

            def sum_direct(direct, lo, half, c, summed):
                nc.vector.tensor_reduce(
                    feats[half * HALF:half * HALF + P - lo, 0 if lo else 1, bass.ds(c * CHUNK_ROWS, CHUNK_ROWS)],
                    direct[lo:P, :].rearrange("p (b d) -> p b d", d=DIM), AX_X, ALU.add).then_inc(summed, 1)

            l0_products(0, 0, PROLOGUE_L0_AT)
            dve.wait_ge(z0_read, 2)
            for t in range(L12_TILES):
                l1_product(0, t, L0_TILES, PROLOGUE_L0_AT + L0_TILES)
                if t == 8:
                    dve.wait_ge(z0_read, 3)
                    sum_direct(direct0, HALF, 0, 0, direct0_summed)

            def l2_products(c, sums):
                dve.wait_ge(z1_read, 3 * c + 2)
                for t in range(L12_TILES):
                    l12_product(t, x2, before_l2(c), L2_AT)
                    if t == 3:
                        dve.wait_ge(z1_read, 3 * c + 3)
                        sum_direct(direct1, HALF, 1, c, direct1_summed)
                    if t == L12_TILES - 1 and sums:
                        dve.wait_ge(z0_read, 3 * c + 6)
                        sum_direct(direct0, HALF, 0, c + 1, direct0_summed)

            def sum2(c):
                dve.wait_ge(z2_read, c + 2)
                sum_direct(direct2, 0, 0, c, direct2_summed)

            with dve.Fori(0, CHUNKS - 1) as c:
                l0_products(c + 1, before_l0(c + 1), L0_AT)
                l2_products(c, True)
                dve.wait_ge(z0_read, 3 * c + 5)
                for t in range(L12_TILES):
                    l1_product(c + 1, t, before_l1(c + 1), L1_AT)
                    if t == LEAD + 4:
                        sum2(c)
            dve.wait_ge(z1_read, 3 * CHUNKS - 1)
            for t in range(L12_TILES):
                l12_product(t, x2, before_l1(CHUNKS - 1) + L12_TILES, 0)
                if t == 3:
                    dve.wait_ge(z1_read, 3 * CHUNKS)
                    sum_direct(direct1, HALF, 1, CHUNKS - 1, direct1_summed)
            sum2(CHUNKS - 1)

        @block.tensor
        def _(pe):
            def select_x(c):
                pe.wait_ge(gathers_done, 16 * SLOTS * (c + 1))
                if not isinstance(c, int) or c > 0:
                    pe.wait_ge(x_copied, c)
                cols = x_bank[0:RF, :].rearrange("p (b d) -> p b d", d=DIM)
                for r in range(REP):
                    k = sum(r < rows for rows in SLOT_ROWS)
                    n = SLOT_ROWS[k - 1] * FIELDS
                    last = nc.tensor.matmul(
                        cols[:, r:r + REP * (k - 1) + 1:REP, :], x_sel[0:n, r, :],
                        gathered[0:n, 0:k * DIM].rearrange("p (i d) -> p i d", d=DIM), start=True, stop=True)
                last.then_inc(x_selected, 1)

            def spread(c, n, after_l0, first):
                if n < L0_TILES:
                    if n == 0:
                        pe.wait_ge(parts_a_ready, c + 1)
                    if n >= SPREAD_BANKS:
                        pe.wait_ge(products_ready, after_l0 + n - SPREAD_BANKS + 1)
                    elif not first:
                        pe.wait_ge(spreads_copied, L12_TILES * c - SPREAD_BANKS + n + 1)
                    m = L0_ROWS[n]
                    lhs, parts = shift_sel[:, n, 0:m], parts_a
                else:
                    t = n - L0_TILES
                    if t == 0:
                        pe.wait_ge(parts_b_ready, c + 1)
                    if t < SPREAD_BANKS:
                        pe.wait_ge(products_ready, after_l0 + n - SPREAD_BANKS + 1)
                    else:
                        pe.wait_ge(spreads_copied, L12_TILES * c + t - SPREAD_BANKS + 1)
                    m = L12_ROWS[t]
                    lhs, parts = field_sel[:, t, 0:m], parts_b
                nc.tensor.matmul(spread_banks[n % SPREAD_BANKS][0:m, :], lhs, parts[:, :],
                                 start=True, stop=True).then_inc(spreads_done, 1)

            def weigh(z, w, rows, t, tiles, made, place, z_ready):
                n = rows[t]
                pe.wait_ge(products_ready, made + t + 1)
                mm = nc.tensor.matmul(z[:, :], w[0:n, t, :], slot(place + t)[0:n, :],
                                      start=(t == 0), stop=(t == tiles - 1))
                mm.then_inc(products_used, 1)
                if t == tiles - 1:
                    pe.wait_ge(products_used, made + tiles)
                    pe.sem_inc(z_ready, 1)

            def layer0(t, made, place):
                weigh(z0, w0_sb, L0_ROWS, t, L0_TILES, made, place, z0_ready)

            def layer1(t, made, place):
                weigh(z1, w1_sb, L12_ROWS, t, L12_TILES, made, place, z1_ready)

            def layer2(t, made, place):
                weigh(z2, w2_sb, L12_ROWS, t, L12_TILES, made, place, z2_ready)

            pe.wait_ge(consts_in, 6 * 16)
            select_x(0)
            done = SPREAD_BANKS
            for n in range(done):
                spread(0, n, 0, True)
            pe.wait_ge(w0_ready, 1)
            for t in range(L0_TILES):
                if done < SPREADS:
                    spread(0, done, 0, True)
                    done += 1
                layer0(t, 0, PROLOGUE_L0_AT)
            pe.wait_ge(w12_in, 4 * 16)
            for t in range(L12_TILES):
                while done < min(SPREADS, L0_TILES + t + LEAD):
                    spread(0, done, 0, True)
                    done += 1
                if t == 10:
                    select_x(1)
                if t >= L12_TILES - LEAD:
                    spread(1, t - (L12_TILES - LEAD), PROLOGUE, False)
                layer1(t, L0_TILES, PROLOGUE_L0_AT + L0_TILES)

            def step(c, more):
                made = before_l0(c + 1)
                pe.wait_ge(z0_read, 3 * (c + 1))
                for t in range(L0_TILES):
                    if LEAD + t < L0_TILES:
                        spread(c + 1, LEAD + t, made, False)
                    layer0(t, made, L0_AT)
                pe.wait_ge(z2_read, c + 1)
                for t in range(L12_TILES):
                    if t == 5 and more:
                        select_x(c + 2)
                    if t >= L12_TILES - LEAD:
                        spread(c + 1, L0_TILES + t - (L12_TILES - LEAD), made, False)
                    layer2(t, before_l2(c), L2_AT)
                pe.wait_ge(z1_read, 3 * (c + 1))
                for t in range(L12_TILES):
                    if LEAD + t < L12_TILES:
                        spread(c + 1, L0_TILES + LEAD + t, made, False)
                    elif more:
                        spread(c + 2, LEAD + t - L12_TILES, before_l0(c + 2), False)
                    layer1(t, before_l1(c + 1), L1_AT)

            with pe.Fori(0, CHUNKS - 2) as c:
                step(c, True)
            step(CHUNKS - 2, False)
            pe.wait_ge(z2_read, CHUNKS)
            for t in range(L12_TILES):
                layer2(t, before_l1(CHUNKS - 1) + L12_TILES, 0)

            pe.wait_ge(tower_in, 7 * 16)
            pe.wait_ge(direct0_summed, CHUNKS)
            pe.wait_ge(direct1_summed, CHUNKS + 1)
            pe.wait_ge(z0_read, 3 * CHUNKS)
            pe.wait_ge(z1_read, 3 * CHUNKS)
            pe.wait_ge(z2_read, CHUNKS + 1)
            pe.wait_ge(direct2_summed, CHUNKS + 1)
            for m in range(HID1 // P):
                cols = slice(m * P, (m + 1) * P)
                nc.tensor.matmul(tower_banks[m][:, :], wt1d_sb[:, cols], dense_sb[:, :], start=True, stop=False)
                nc.tensor.matmul(tower_banks[m][:, :], wt1_sb[:, 0, cols], feats[:, 0, :], start=False, stop=False)
                nc.tensor.matmul(tower_banks[m][:, :], wt1_sb[:, 1, cols], feats[:, 1, :],
                                 start=False, stop=True).then_inc(tower_mm, 1)
            for a in range(HID1 // P):
                pe.wait_ge(tower_act, a + 1)
                for m in range(HID2 // P):
                    mm = nc.tensor.matmul(tower_banks[HID1 // P + m][:, :], wt2_sb[:, a, m * P:(m + 1) * P],
                                          hid1[:, a, :], start=(a == 0), stop=(a == HID1 // P - 1))
                    if a == HID1 // P - 1:
                        mm.then_inc(tower_mm, 1)
            for m in range(HID2 // P):
                pe.wait_ge(tower_act, HID1 // P + m + 1)
                mm = nc.tensor.matmul(y_bank[0:1, :], wt3_sb[:, m:m + 1], hid2[:, m, :],
                                      start=(m == 0), stop=(m == HID2 // P - 1))
            mm.then_inc(tower_mm, 1)


def kernel(**inputs):
    import ml_dtypes
    import concourse.bacc as bacc
    from concourse.bass_utils import run_bass_kernel_spmd

    def arr(name):
        return np.ascontiguousarray(inputs[name])

    tables = [arr(f"tbl_{f}") for f in range(FIELDS)]
    starts = np.cumsum([0] + [t.shape[0] for t in tables[:-1]]).astype(np.int32)
    ids = arr("ids").astype(np.int32)

    padded = np.zeros((CHUNKS, SLOTS * REP, FIELDS), np.int32)
    padded[:, :CHUNK_ROWS] = ids.reshape(CHUNKS, CHUNK_ROWS, FIELDS)
    ids_laid = np.ascontiguousarray(
        padded.reshape(CHUNKS, SLOTS, REP, FIELDS).transpose(2, 3, 0, 1).reshape(RF, CHUNKS * SLOTS))
    bases = np.ascontiguousarray(np.tile(starts, REP)[:, None] + np.zeros((RF, CHUNKS * SLOTS), np.int32))

    f = np.arange(FIELDS)
    x_select = np.zeros((RF, REP, RF), np.float32)
    for r in range(REP):
        for q in range(REP):
            x_select[r * FIELDS + f, r, q * FIELDS + f] = 1
    shift_select = np.zeros((RF, L0_TILES, RF), ml_dtypes.bfloat16)
    field_select = np.zeros((RF, L12_TILES, P), ml_dtypes.bfloat16)
    for part in range(REP):
        for s in range(SHIFTS):
            shift_select[part * FIELDS + (f + s) % FIELDS, s // REP, s % REP * FIELDS + f] = 1
        for h in range(FIELDS):
            field_select[part * FIELDS + h, h // 2, h % 2 * HALF:(h % 2 + 1) * HALF] = 1

    w0 = arr("L0_rec_w0")
    upper = np.zeros((L0_TILES * REP, FIELDS, MAPS), np.float32)
    lower = np.zeros_like(upper)
    for s in range(SHIFTS):
        upper[s] = w0[f, (f + s) % FIELDS]
        if s:
            lower[s] = w0[(f + s) % FIELDS, f]

    def tiled(w):
        return np.ascontiguousarray(w.reshape(L0_TILES, RF, MAPS).transpose(1, 0, 2))

    def column(name, parts):
        return np.ascontiguousarray(arr(name).reshape(parts, P).T)

    feeds = {
        "tables": np.concatenate(tables, axis=0),
        "ids": ids_laid,
        "bases": bases,
        "x_select": x_select,
        "shift_select": shift_select,
        "field_select": field_select,
        "w0_upper": tiled(upper),
        "w0_lower": tiled(lower),
        "w1": arr("L0_rec_w1").reshape(FIELDS * HALF, MAPS),
        "w2": arr("L0_rec_w2").reshape(FIELDS * HALF, MAPS),
        "b0": column("L0_rec_b0", 1),
        "b1": column("L0_rec_b1", 1),
        "b2": column("L0_rec_b2", 1),
        "dense_t": np.ascontiguousarray(arr("dense_ctx").T),
        "w_top1": arr("W_top1"),
        "b_top1": column("b_top1", HID1 // P),
        "w_top2": arr("W_top2"),
        "b_top2": column("b_top2", HID2 // P),
        "w_top3": column("W_top3", HID2 // P),
    }
    nc = bacc.Bacc("TRN2", target_bir_lowering=False, num_devices=1)
    args = [nc.dram_tensor(f"in_{k}", a.shape, mybir.dt.from_np(a.dtype), kind="ExternalInput").ap()
            for k, a in feeds.items()]
    args.append(nc.dram_tensor("out_y", (1, BATCH), F32, kind="ExternalOutput").ap())
    interaction_tower(nc, *args)
    r = run_bass_kernel_spmd(nc, [{f"in_{k}": a for k, a in feeds.items()}], core_ids=[0])
    return r.results[0]["out_y"].reshape(BATCH, 1)
```

```python
from contextlib import ExitStack

import numpy as np

import concourse.bass as bass
from concourse import mybir

F32 = mybir.dt.float32
F32R = mybir.dt.float32r
I32 = mybir.dt.int32
ALU = mybir.AluOpType
ACT = mybir.ActivationFunctionType
AX_X = mybir.AxisListType.X

BATCH = 512
FIELDS = 39
DIM = 16
MAPS = 128
HALF = MAPS // 2
DENSE = 16
HID1, HID2 = 512, 256
P = 128

CHUNK_ROWS = 32
COLS = CHUNK_ROWS * DIM
CHUNKS = BATCH // CHUNK_ROWS

REP = 3
RF = REP * FIELDS
SLOTS = -(-CHUNK_ROWS // REP)
SLOT_ROWS = [min(REP, CHUNK_ROWS - REP * i) for i in range(SLOTS)]
STORED_ROWS = 64

SHIFTS = (FIELDS + 1) // 2
L0_TILES = -(-SHIFTS // REP)
L0_ROWS = [min(REP, SHIFTS - REP * j) * FIELDS for j in range(L0_TILES)]
L12_TILES = -(-FIELDS // 2)
L12_ROWS = [min(2, FIELDS - 2 * t) * HALF for t in range(L12_TILES)]
assert FIELDS + REP * (L0_TILES - 1) + REP - 1 <= STORED_ROWS and 2 * L12_TILES <= STORED_ROWS

GROUP = 2
L0_GROUPS = -(-L0_TILES // GROUP)
L12_GROUPS = L12_TILES // GROUP
GROUPS = L0_GROUPS + 2 * L12_GROUPS
PROLOGUE = L0_GROUPS + L12_GROUPS
PRODUCT_SLOTS = 8
assert GROUPS % PRODUCT_SLOTS == 0
L0_AT, L2_AT, L1_AT = 0, L0_GROUPS, L0_GROUPS + L12_GROUPS
PROLOGUE_AT = GROUPS - PROLOGUE

SPLIT = (1, 3, 5, 7)
SPLITS = 2 * len(SPLIT)
PART_SLOTS = 4
assert SPLITS % PART_SLOTS == 0

LOAD_TILES = 4
LOADS = L12_TILES // LOAD_TILES


def interaction_tower(nc, tables, ids, bases, x_select,
                      w0_upper, w0_lower, w1, w2, b0, b1, b2,
                      dense_t, w_top1, b_top1, w_top2, b_top2, w_top3, out):
    ctx = ExitStack()
    with ctx:
        def sb(name, shape, dt=F32):
            return ctx.enter_context(nc.sbuf_tensor(name, shape, dt))

        def bank(name):
            return ctx.enter_context(nc.psum_tensor(name, [P, COLS], F32))

        def sem(name):
            return ctx.enter_context(nc.semaphore(name))

        x_dram = nc.dram_tensor("x_dram", (CHUNKS, STORED_ROWS, COLS), F32, kind="Internal").ap()

        ids_sb = sb("ids_sb", [RF, CHUNKS * SLOTS], I32)
        bases_sb = sb("bases_sb", [RF, CHUNKS * SLOTS], I32)
        rows_sb = sb("rows_sb", [RF, CHUNKS * SLOTS], I32)
        x_sel = sb("x_sel", [RF, REP, RF])
        w0_sb = sb("w0_sb", [RF, L0_TILES, MAPS])
        w1_sb = sb("w1_sb", [P, L12_TILES, MAPS])
        w2_sb = sb("w2_sb", [P, L12_TILES, MAPS])
        w1_hi = sb("w1_hi", [P, len(SPLIT) * GROUP, MAPS], F32R)
        w1_lo = sb("w1_lo", [P, len(SPLIT) * GROUP, MAPS], F32R)
        w2_hi = sb("w2_hi", [P, len(SPLIT) * GROUP, MAPS], F32R)
        w2_lo = sb("w2_lo", [P, len(SPLIT) * GROUP, MAPS], F32R)
        bias_sb = sb("bias_sb", [P, 3])
        wt1_sb = sb("wt1_sb", [P, 2, HID1])
        wt1d_sb = sb("wt1d_sb", [DENSE, HID1])
        bt1_sb = sb("bt1_sb", [P, HID1 // P])
        wt2_sb = sb("wt2_sb", [P, HID1 // P, HID2])
        bt2_sb = sb("bt2_sb", [P, HID2 // P])
        wt3_sb = sb("wt3_sb", [P, HID2 // P])
        dense_sb = sb("dense_sb", [DENSE, BATCH])

        rows_now = sb("rows_now", [RF, SLOTS], I32)
        gathered = sb("gathered", [RF, SLOTS * DIM])
        x_rep = sb("x_rep", [RF, COLS])
        x_shifted = sb("x_shifted", [RF, L0_TILES, COLS])
        x_spread = sb("x_spread", [P, L12_TILES, COLS])
        products = sb("products", [P, PRODUCT_SLOTS, GROUP, COLS])
        parts_hi = sb("parts_hi", [P, PART_SLOTS, GROUP, COLS], F32R)
        parts_lo = sb("parts_lo", [P, PART_SLOTS, GROUP, COLS], F32R)
        x1 = sb("x1", [P, COLS])
        x2 = sb("x2", [P, COLS])
        direct0 = sb("direct0", [P, COLS])
        direct1 = sb("direct1", [P, COLS])
        direct2 = sb("direct2", [P, COLS])
        feats = sb("feats", [P, 2, BATCH])
        y_sb = sb("y_sb", [1, BATCH])
        w0l_sb = x_spread[0:RF, 0:2, :].rearrange("p a n -> p (a n)")[:, 0:L0_TILES * MAPS].rearrange(
            "p (j s) -> p j s", s=MAPS)
        hid1 = products[:, 0:2, :, :].rearrange("p a b n -> p (a b) n")
        hid2 = products[:, 2, :, :]

        x_bank = bank("x_bank")
        z0, z1, z2 = bank("z0"), bank("z1"), bank("z2")
        tower_banks = [bank(f"tower{n}") for n in range(4)]
        hid1_banks = tower_banks
        hid2_banks = [z0, z1]
        y_bank = z2

        ids_in = sem("ids_in")
        consts_in = sem("consts_in")
        w0_in = sem("w0_in")
        w12_in = sem("w12_in")
        tower_in = sem("tower_in")
        pool_waits = sem("pool_waits")
        rows_known = sem("rows_known")
        w0_ready = sem("w0_ready")
        w_hi_ready = sem("w_hi_ready")
        w_lo_ready = sem("w_lo_ready")
        rows_copied = sem("rows_copied")
        gathers_done = sem("gathers_done")
        x_selected = sem("x_selected")
        x_copied = sem("x_copied")
        x_stored = sem("x_stored")
        x_shifted_in = sem("x_shifted_in")
        x_spread_in = [sem(f"x_spread_in{q}") for q in range(LOADS)]
        products_made = sem("products_made")
        his_made = sem("his_made")
        los_made = sem("los_made")
        groups_used = sem("groups_used")
        z0_read = sem("z0_read")
        z1_read = sem("z1_read")
        z2_read = sem("z2_read")
        direct0_summed = sem("direct0_summed")
        direct1_summed = sem("direct1_summed")
        direct2_summed = sem("direct2_summed")
        tower_mm = sem("tower_mm")
        tower_act = sem("tower_act")
        stored = sem("stored")

        block = ctx.enter_context(nc.Block())

        def group(c, place):
            return GROUPS * (c + 1) - PROLOGUE_AT + place

        def split(c, rank):
            return SPLITS * (c + 1) - SPLITS // 2 + rank

        SPLIT_PLACES = [L2_AT + g for g in SPLIT] + [L1_AT + g for g in SPLIT]

        def since(count, semaphore, eng):
            if not isinstance(count, int) or count > 0:
                eng.wait_ge(semaphore, count)

        @block.sync
        def _(sp):
            sp.dma_start(ids_sb[:, :], ids).then_inc(ids_in, 16)
            sp.dma_start(bases_sb[:, :], bases).then_inc(ids_in, 16)
            sp.dma_start(x_sel[:, :, :], x_select).then_inc(consts_in, 16)
            sp.dma_start(w0_sb[:, :, :], w0_upper).then_inc(w0_in, 16)
            sp.dma_start(w0l_sb, w0_lower).then_inc(w0_in, 16)
            sp.dma_start(bias_sb[:, 0:1], b0).then_inc(consts_in, 16)
            sp.dma_start(bias_sb[:, 1:2], b1).then_inc(consts_in, 16)
            sp.dma_start(bias_sb[:, 2:3], b2).then_inc(consts_in, 16)
            whole = (L12_TILES - 1) * P
            for w_sb, w in ((w1_sb, w1), (w2_sb, w2)):
                sp.dma_start(w_sb[:, 0:L12_TILES - 1, :],
                             w[0:whole, :].rearrange("(t p) s -> p t s", p=P)).then_inc(w12_in, 16)
                sp.dma_start(w_sb[0:HALF, L12_TILES - 1, :], w[whole:whole + HALF, :]).then_inc(w12_in, 16)

            def store_x(c):
                sp.wait_ge(x_copied, c + 1)
                sp.dma_start(x_dram[c], x_rep[0:STORED_ROWS, :]).then_inc(x_stored, 16)
                sp.wait_ge(x_stored, 16 * (c + 1))

            def load_shifted(c):
                for r in range(REP):
                    tiles = len(range(r, SHIFTS, REP))
                    src = x_dram[c, r:r + FIELDS, :]
                    sp.dma_start(
                        x_shifted[r * FIELDS:(r + 1) * FIELDS, 0:tiles, :],
                        bass.AP(tensor=src.tensor, offset=src.offset,
                                ap=[[COLS, FIELDS], [REP * COLS, tiles], [1, COLS]])).then_inc(x_shifted_in, 16)

            def load_spread(c, q):
                t0 = q * LOAD_TILES
                for i in range(2):
                    src = x_dram[c, 2 * t0 + i:2 * (t0 + LOAD_TILES - 1) + i + 1:2, :]
                    sp.dma_start(x_spread[i * HALF:(i + 1) * HALF, t0:t0 + LOAD_TILES, :],
                                 src.partition_broadcast(HALF)).then_inc(x_spread_in[q], 16)

            store_x(0)
            load_shifted(0)
            sp.wait_ge(w0_ready, 1)
            for q in range(LOADS):
                load_spread(0, q)
            sp.dma_start(wt1_sb[:, :, :], w_top1[0:2 * P, :].rearrange("(a p) m -> p a m", p=P)).then_inc(tower_in, 16)
            sp.dma_start(wt1d_sb[:, :], w_top1[2 * P:2 * P + DENSE, :]).then_inc(tower_in, 16)
            sp.dma_start(wt2_sb[:, :, :], w_top2.rearrange("(a p) m -> p a m", p=P)).then_inc(tower_in, 16)
            sp.dma_start(bt1_sb[:, :], b_top1).then_inc(tower_in, 16)
            sp.dma_start(bt2_sb[:, :], b_top2).then_inc(tower_in, 16)
            sp.dma_start(wt3_sb[:, :], w_top3).then_inc(tower_in, 16)
            sp.dma_start(dense_sb[:, :], dense_t).then_inc(tower_in, 16)
            store_x(1)
            sp.wait_ge(products_made, L0_GROUPS)
            load_shifted(1)

            def turn(c, more):
                if more:
                    store_x(c + 2)
                    sp.wait_ge(products_made, group(c, L2_AT))
                    load_shifted(c + 2)
                for q in range(LOADS):
                    sp.wait_ge(products_made, group(c, L2_AT + (q + 1) * LOAD_TILES // GROUP))
                    load_spread(c + 1, q)

            with sp.Fori(0, CHUNKS - 2) as c:
                turn(c, True)
            turn(CHUNKS - 2, False)
            sp.wait_ge(tower_act, HID1 // P + HID2 // P + 1)
            sp.dma_start(out, y_sb[:, :]).then_inc(stored, 16)
            sp.wait_ge(stored, 16)

        @block.gpsimd
        def _(pool):
            def wait(semaphore, count):
                pool.wait_ge(semaphore, count)
                pool.sem_inc(pool_waits, 1)

            def gather(c):
                nc.gpsimd.tensor_copy(rows_now[:, :], rows_sb[:, bass.ds(c * SLOTS, SLOTS)]).then_inc(rows_copied, 1)
                wait(rows_copied, c + 1)
                for i in range(SLOTS):
                    n = SLOT_ROWS[i] * FIELDS
                    nc.gpsimd.indirect_dma_start(
                        out=gathered[0:n, i * DIM:(i + 1) * DIM], out_offset=None, in_=tables,
                        in_offset=bass.IndirectOffsetOnAxis(ap=rows_now[0:n, i:i + 1], axis=0),
                    ).then_inc(gathers_done, 16)

            wait(rows_known, 1)
            gather(0)
            with pool.Fori(1, CHUNKS) as c:
                wait(x_selected, c)
                gather(c)

        @block.scalar
        def _(act):
            def copy_x(c):
                act.wait_ge(x_selected, c + 1)
                if not isinstance(c, int) or c > 0:
                    act.wait_ge(products_made, group(c - 2, L2_AT) if not isinstance(c, int) or c > 1
                                else L0_GROUPS)
                    act.wait_ge(x_stored, 16 * c)
                nc.scalar.activation(x_rep[:, :], x_bank[0:RF, :], ACT.Copy).then_inc(x_copied, 1)

            def layer_out(z, z_made, z_read, x_next, x_used, direct, sums, bias_at):
                act.wait_ge(groups_used, z_made)
                since(x_used, products_made, act)
                bias = bias_sb[:, bias_at:bias_at + 1]
                nc.scalar.activation(x_next[0:HALF, :], z[0:HALF, :], ACT.Relu, bias=bias[0:HALF]).then_inc(z_read, 1)
                nc.scalar.activation(x_next[HALF:P, :], z[0:HALF, :], ACT.Relu, bias=bias[0:HALF]).then_inc(z_read, 1)
                act.wait_ge(*sums)
                nc.scalar.activation(direct[HALF:P, :], z[HALF:P, :], ACT.Relu, bias=bias[HALF:P]).then_inc(z_read, 1)

            def layer0_out(c):
                layer_out(z0, group(c, L2_AT) if not isinstance(c, int) or c >= 0 else L0_GROUPS, z0_read,
                          x1, group(c, 0) if not isinstance(c, int) or c >= 0 else 0,
                          direct0, (direct0_summed, c + 2), 0)

            def layer1_out(c):
                layer_out(z1, group(c, 0), z1_read, x2, group(c - 1, L1_AT), direct1, (direct1_summed, c + 1), 1)

            def layer2_out(c, at=L2_AT):
                act.wait_ge(groups_used, group(c, at + L12_GROUPS))
                act.wait_ge(direct2_summed, c + 1)
                nc.scalar.activation(direct2[:, :], z2[:, :], ACT.Relu, bias=bias_sb[:, 2:3]).then_inc(z2_read, 1)

            def high_part(c, rank, shift=0):
                place = SPLIT_PLACES[rank] - shift
                act.wait_ge(products_made, group(c, place) + 1)
                if rank >= PART_SLOTS:
                    if not isinstance(c, int) or c >= 0:
                        act.wait_ge(groups_used, group(c, SPLIT_PLACES[rank - PART_SLOTS]) + 1)
                else:
                    act.wait_ge(groups_used, group(c - 1, SPLIT_PLACES[rank + SPLITS - PART_SLOTS]) + 1)
                nc.scalar.activation(parts_hi[:, rank % PART_SLOTS, :, :], products[:, place % PRODUCT_SLOTS, :, :],
                                     ACT.Copy).then_inc(his_made, 1)

            act.sem_inc(z2_read, 1)
            act.wait_ge(consts_in, 4 * 16)
            copy_x(0)
            act.wait_ge(w12_in, 4 * 16)
            for w_sb, w_hi in ((w1_sb, w1_hi), (w2_sb, w2_hi)):
                for n, g in enumerate(SPLIT):
                    nc.scalar.activation(w_hi[:, GROUP * n:GROUP * (n + 1), :], w_sb[:, GROUP * g:GROUP * (g + 1), :],
                                         ACT.Copy).then_inc(w_hi_ready, 1)
            copy_x(1)
            layer0_out(-1)
            for rank in range(SPLITS // 2, SPLITS):
                high_part(-1, rank)

            def turn(c, more):
                layer1_out(c)
                if more:
                    copy_x(c + 2)
                for rank in range(SPLITS // 2):
                    high_part(c, rank)
                    if rank == 1:
                        layer0_out(c)
                for rank in range(SPLITS // 2, SPLITS):
                    high_part(c, rank)
                layer2_out(c)

            with act.Fori(0, CHUNKS - 2) as c:
                turn(c, True)
            turn(CHUNKS - 2, False)
            layer1_out(CHUNKS - 1)
            for rank in range(SPLITS // 2):
                high_part(CHUNKS - 1, rank, L2_AT)
            layer2_out(CHUNKS - 1, 0)

            act.wait_ge(tower_in, 7 * 16)
            for m in range(HID1 // P):
                act.wait_ge(tower_mm, m + 1)
                nc.scalar.activation(hid1[:, m, :], hid1_banks[m][:, :], ACT.Relu,
                                     bias=bt1_sb[:, m:m + 1]).then_inc(tower_act, 1)
            for m in range(HID2 // P):
                act.wait_ge(tower_mm, HID1 // P + m + 1)
                nc.scalar.activation(hid2[:, m, :], hid2_banks[m][:, :], ACT.Relu,
                                     bias=bt2_sb[:, m:m + 1]).then_inc(tower_act, 1)
            act.wait_ge(tower_mm, HID1 // P + HID2 // P + 1)
            nc.scalar.activation(y_sb[:, :], y_bank[0:1, :], ACT.Copy).then_inc(tower_act, 1)

        @block.vector
        def _(dve):
            dve.sem_inc(direct0_summed, 1)
            dve.sem_inc(direct1_summed, 1)
            dve.sem_inc(direct2_summed, 1)
            dve.wait_ge(ids_in, 2 * 16)
            nc.vector.tensor_tensor(rows_sb[:, :], ids_sb[:, :], bases_sb[:, :], ALU.add).then_inc(rows_known, 1)
            dve.wait_ge(w0_in, 2 * 16)
            nc.vector.tensor_tensor(w0_sb[:, :, :], w0_sb[:, :, :], w0l_sb, ALU.add).then_inc(w0_ready, 1)
            for k, (w_sb, w_hi, w_lo) in enumerate(((w1_sb, w1_hi, w1_lo), (w2_sb, w2_hi, w2_lo))):
                for n, g in enumerate(SPLIT):
                    dve.wait_ge(w_hi_ready, k * len(SPLIT) + n + 1)
                    part = slice(GROUP * n, GROUP * (n + 1))
                    nc.vector.tensor_tensor(w_lo[:, part, :], w_sb[:, GROUP * g:GROUP * (g + 1), :],
                                            w_hi[:, part, :].bitcast(F32), ALU.subtract).then_inc(w_lo_ready, 1)

            def multiply(c, place, tiles, spread, x):
                since(group(c, place) - PRODUCT_SLOTS + 1, groups_used, dve)
                n = spread.shape[0]
                nc.vector.tensor_tensor(products[0:n, place % PRODUCT_SLOTS, 0:tiles, :], spread,
                                        x[0:n, :].unsqueeze(1).to_broadcast([n, tiles, COLS]),
                                        ALU.mult).then_inc(products_made, 1)

            def layer0_products(c, at=L0_AT):
                dve.wait_ge(x_copied, c + 2)
                dve.wait_ge(x_shifted_in, 16 * REP * (c + 2))
                for g in range(L0_GROUPS):
                    t0, t1 = g * GROUP, min((g + 1) * GROUP, L0_TILES)
                    multiply(c, at + g, t1 - t0, x_shifted[0:min(L0_ROWS[t0:t1]), t0:t1, :], x_rep)

            def low_part(c, rank, shift=0):
                place = SPLIT_PLACES[rank] - shift
                dve.wait_ge(his_made, split(c, rank) + 1)
                nc.vector.tensor_tensor(parts_lo[:, rank % PART_SLOTS, :, :], products[:, place % PRODUCT_SLOTS, :, :],
                                        parts_hi[:, rank % PART_SLOTS, :, :].bitcast(F32),
                                        ALU.subtract).then_inc(los_made, 1)

            def layer_products(c, at, x, first_rank, loaded, shift, sums):
                for g in range(L12_GROUPS):
                    if loaded is not None and g % (LOAD_TILES // GROUP) == 0:
                        dve.wait_ge(x_spread_in[g * GROUP // LOAD_TILES], 2 * 16 * loaded)
                    multiply(c, at + g, GROUP, x_spread[:, g * GROUP:(g + 1) * GROUP, :], x)
                    if g - 1 in SPLIT:
                        low_part(c, first_rank + SPLIT.index(g - 1), shift)
                    if g in sums:
                        sums[g]()

            def layer1_products(c, sums):
                dve.wait_ge(z0_read, 3 * (c + 1) + 2)
                layer_products(c, L1_AT, x1, SPLITS // 2, c + 2, 0, sums)

            def layer2_products(c, sums, at=L2_AT):
                dve.wait_ge(z1_read, 3 * c + 2)
                layer_products(c, at, x2, 0, None, L2_AT - at, sums)

            def sum_direct(direct, to, half, c, summed):
                lo, n = (0, P) if half == 1 else (HALF, HALF)
                nc.vector.tensor_reduce(
                    feats[to:to + n, half, bass.ds(c * CHUNK_ROWS, CHUNK_ROWS)],
                    direct[lo:P, :].rearrange("p (b d) -> p b d", d=DIM), AX_X, ALU.add).then_inc(summed, 1)

            def sum0(c):
                dve.wait_ge(z0_read, 3 * c + 3)
                sum_direct(direct0, 0, 0, c, direct0_summed)

            def sum1(c):
                dve.wait_ge(z1_read, 3 * c + 3)
                sum_direct(direct1, HALF, 0, c, direct1_summed)

            def sum2(c):
                dve.wait_ge(z2_read, c + 2)
                sum_direct(direct2, 0, 1, c, direct2_summed)

            layer0_products(-1, PROLOGUE_AT)
            layer1_products(-1, {4: lambda: sum0(0)})
            with dve.Fori(0, CHUNKS - 1) as c:
                layer0_products(c)
                layer2_products(c, {2: lambda: sum1(c), L12_GROUPS - 1: lambda: sum0(c + 1)})
                layer1_products(c, {L12_GROUPS - 1: lambda: sum2(c)})
            layer2_products(CHUNKS - 1, {2: lambda: sum1(CHUNKS - 1)}, 0)
            sum2(CHUNKS - 1)

        @block.tensor
        def _(pe):
            def select_x(c):
                pe.wait_ge(gathers_done, 16 * SLOTS * (c + 1))
                since(c, x_copied, pe)
                cols = x_bank[0:RF, :].rearrange("p (b d) -> p b d", d=DIM)
                for r in range(REP):
                    k = sum(r < rows for rows in SLOT_ROWS)
                    n = SLOT_ROWS[k - 1] * FIELDS
                    last = nc.tensor.matmul(
                        cols[:, r:r + REP * (k - 1) + 1:REP, :], x_sel[0:n, r, :],
                        gathered[0:n, 0:k * DIM].rearrange("p (i d) -> p i d", d=DIM), start=True, stop=True)
                last.then_inc(x_selected, 1)

            def layer0(c, at=L0_AT, between=None):
                for g in range(L0_GROUPS):
                    pe.wait_ge(products_made, group(c, at + g) + 1)
                    for t in range(g * GROUP, min((g + 1) * GROUP, L0_TILES)):
                        n = L0_ROWS[t]
                        last = nc.tensor.matmul(z0[:, :], w0_sb[0:n, t, :],
                                                products[0:n, (at + g) % PRODUCT_SLOTS, t % GROUP, :],
                                                start=(t == 0), stop=(t == L0_TILES - 1))
                    last.then_inc(groups_used, 1)
                    if g == 1 and between is not None:
                        between()

            def layer(c, at, z, w, w_hi, w_lo, first_rank):
                for g in range(L12_GROUPS):
                    place = (at + g) % PRODUCT_SLOTS
                    if g in SPLIT:
                        n = SPLIT.index(g)
                        rank = first_rank + n
                        pe.wait_ge(los_made, split(c, rank) + 1)
                        for i in range(GROUP):
                            hi = parts_hi[:, rank % PART_SLOTS, i, :]
                            lo = parts_lo[:, rank % PART_SLOTS, i, :]
                            for a, b in ((w_hi, hi), (w_lo, hi), (w_hi, lo)):
                                last = nc.tensor.matmul(z[:, :], a[:, GROUP * n + i, :], b, start=False, stop=False)
                    else:
                        pe.wait_ge(products_made, group(c, at + g) + 1)
                        for t in range(g * GROUP, (g + 1) * GROUP):
                            n = L12_ROWS[t]
                            last = nc.tensor.matmul(z[:, :], w[0:n, t, :], products[0:n, place, t % GROUP, :],
                                                    start=(t == 0), stop=(t == L12_TILES - 1))
                    last.then_inc(groups_used, 1)

            def layer1(c):
                layer(c, L1_AT, z1, w1_sb, w1_hi, w1_lo, SPLITS // 2)

            def layer2(c, at=L2_AT):
                layer(c, at, z2, w2_sb, w2_hi, w2_lo, 0)

            pe.wait_ge(consts_in, 4 * 16)
            select_x(0)
            pe.wait_ge(w0_ready, 1)
            select_x(1)
            layer0(-1, PROLOGUE_AT)
            pe.wait_ge(w12_in, 4 * 16)
            pe.wait_ge(w_lo_ready, 2 * len(SPLIT))
            layer1(-1)

            def turn(c, more):
                pe.wait_ge(z0_read, 3 * (c + 1))
                layer0(c, L0_AT, (lambda: select_x(c + 2)) if more else None)
                pe.wait_ge(z2_read, c + 1)
                layer2(c)
                pe.wait_ge(z1_read, 3 * (c + 1))
                layer1(c)

            with pe.Fori(0, CHUNKS - 2) as c:
                turn(c, True)
            turn(CHUNKS - 2, False)
            pe.wait_ge(z2_read, CHUNKS)
            layer2(CHUNKS - 1, 0)

            pe.wait_ge(tower_in, 7 * 16)
            pe.wait_ge(direct0_summed, CHUNKS + 1)
            pe.wait_ge(direct1_summed, CHUNKS + 1)
            pe.wait_ge(z0_read, 3 * CHUNKS)
            pe.wait_ge(z1_read, 3 * CHUNKS)
            for m in range(HID1 // P):
                cols = slice(m * P, (m + 1) * P)
                nc.tensor.matmul(hid1_banks[m][:, :], wt1d_sb[:, cols], dense_sb[:, :], start=True, stop=False)
                nc.tensor.matmul(hid1_banks[m][:, :], wt1_sb[:, 0, cols], feats[:, 0, :], start=False, stop=False)
            pe.wait_ge(z2_read, CHUNKS + 1)
            pe.wait_ge(direct2_summed, CHUNKS + 1)
            for m in range(HID1 // P):
                cols = slice(m * P, (m + 1) * P)
                nc.tensor.matmul(hid1_banks[m][:, :], wt1_sb[:, 1, cols], feats[:, 1, :],
                                 start=False, stop=True).then_inc(tower_mm, 1)
            for a in range(HID1 // P):
                pe.wait_ge(tower_act, a + 1)
                for m in range(HID2 // P):
                    mm = nc.tensor.matmul(hid2_banks[m][:, :], wt2_sb[:, a, m * P:(m + 1) * P],
                                          hid1[:, a, :], start=(a == 0), stop=(a == HID1 // P - 1))
                    if a == HID1 // P - 1:
                        mm.then_inc(tower_mm, 1)
            for m in range(HID2 // P):
                pe.wait_ge(tower_act, HID1 // P + m + 1)
                mm = nc.tensor.matmul(y_bank[0:1, :], wt3_sb[:, m:m + 1], hid2[:, m, :],
                                      start=(m == 0), stop=(m == HID2 // P - 1))
            mm.then_inc(tower_mm, 1)


def kernel(**inputs):
    import concourse.bacc as bacc
    from concourse.bass_utils import run_bass_kernel_spmd

    def arr(name):
        return np.ascontiguousarray(inputs[name])

    tables = [arr(f"tbl_{f}") for f in range(FIELDS)]
    starts = np.cumsum([0] + [t.shape[0] for t in tables[:-1]]).astype(np.int32)
    ids = arr("ids").astype(np.int32)

    padded = np.zeros((CHUNKS, SLOTS * REP, FIELDS), np.int32)
    padded[:, :CHUNK_ROWS] = ids.reshape(CHUNKS, CHUNK_ROWS, FIELDS)
    ids_laid = np.ascontiguousarray(
        padded.reshape(CHUNKS, SLOTS, REP, FIELDS).transpose(2, 3, 0, 1).reshape(RF, CHUNKS * SLOTS))
    bases = np.ascontiguousarray(np.tile(starts, REP)[:, None] + np.zeros((RF, CHUNKS * SLOTS), np.int32))

    f = np.arange(FIELDS)
    x_select = np.zeros((RF, REP, RF), np.float32)
    for r in range(REP):
        for q in range(REP):
            x_select[r * FIELDS + f, r, q * FIELDS + f] = 1

    w0 = arr("L0_rec_w0")
    upper = np.zeros((L0_TILES * REP, FIELDS, MAPS), np.float32)
    lower = np.zeros_like(upper)
    for s in range(SHIFTS):
        upper[s] = w0[f, (f + s) % FIELDS]
        if s:
            lower[s] = w0[(f + s) % FIELDS, f]

    def tiled(w):
        return np.ascontiguousarray(w.reshape(L0_TILES, RF, MAPS).transpose(1, 0, 2))

    def column(name, parts):
        return np.ascontiguousarray(arr(name).reshape(parts, P).T)

    feeds = {
        "tables": np.concatenate(tables, axis=0),
        "ids": ids_laid,
        "bases": bases,
        "x_select": x_select,
        "w0_upper": tiled(upper),
        "w0_lower": tiled(lower),
        "w1": arr("L0_rec_w1").reshape(FIELDS * HALF, MAPS),
        "w2": arr("L0_rec_w2").reshape(FIELDS * HALF, MAPS),
        "b0": column("L0_rec_b0", 1),
        "b1": column("L0_rec_b1", 1),
        "b2": column("L0_rec_b2", 1),
        "dense_t": np.ascontiguousarray(arr("dense_ctx").T),
        "w_top1": arr("W_top1"),
        "b_top1": column("b_top1", HID1 // P),
        "w_top2": arr("W_top2"),
        "b_top2": column("b_top2", HID2 // P),
        "w_top3": column("W_top3", HID2 // P),
    }
    nc = bacc.Bacc("TRN2", target_bir_lowering=False, num_devices=1)
    args = [nc.dram_tensor(f"in_{k}", a.shape, mybir.dt.from_np(a.dtype), kind="ExternalInput").ap()
            for k, a in feeds.items()]
    args.append(nc.dram_tensor("out_y", (1, BATCH), F32, kind="ExternalOutput").ap())
    interaction_tower(nc, *args)
    r = run_bass_kernel_spmd(nc, [{f"in_{k}": a for k, a in feeds.items()}], core_ids=[0])
    return r.results[0]["out_y"].reshape(BATCH, 1)
```

```python
from contextlib import ExitStack

import numpy as np

import concourse.bass as bass
from concourse import mybir

F32 = mybir.dt.float32
F32R = mybir.dt.float32r
I32 = mybir.dt.int32
ALU = mybir.AluOpType
ACT = mybir.ActivationFunctionType
AX_X = mybir.AxisListType.X

BATCH = 512
FIELDS = 39
DIM = 16
MAPS = 128
HALF = MAPS // 2
DENSE = 16
HID1, HID2 = 512, 256
P = 128

CHUNK_ROWS = 32
COLS = CHUNK_ROWS * DIM
CHUNKS = BATCH // CHUNK_ROWS

REP = 3
RF = REP * FIELDS
SLOTS = -(-CHUNK_ROWS // REP)
STORED_ROWS = 64

SHIFTS = (FIELDS + 1) // 2
L0_TILES = -(-SHIFTS // REP)
L0_ROWS = [min(REP, SHIFTS - REP * j) * FIELDS for j in range(L0_TILES)]
L12_TILES = -(-FIELDS // 2)
PAIRED_TILE = 4
TILE_FIELDS = [(f, f + 1) for f in range(0, FIELDS - 1, 2)]
TILE_FIELDS.insert(PAIRED_TILE, (FIELDS - 1, FIELDS - 1))
assert FIELDS + REP * (L0_TILES - 1) + REP - 1 <= STORED_ROWS and L12_TILES == len(TILE_FIELDS)

LOAD_TILES = 4

GROUP = 2
L0_GROUPS = -(-L0_TILES // GROUP)
L12_GROUPS = L12_TILES // GROUP
GROUPS = L0_GROUPS + 2 * L12_GROUPS
PROLOGUE = L0_GROUPS + L12_GROUPS
PRODUCT_SLOTS = 8
assert GROUPS % PRODUCT_SLOTS == 0
L0_AT, L2_AT, L1_AT = 0, L0_GROUPS, L0_GROUPS + L12_GROUPS
PROLOGUE_AT = GROUPS - PROLOGUE

SPLIT = {0: (0, 1, 2), 2: (1, 3, 5, 7, 9), 1: (1, 3, 5, 7)}
PAIRED_GROUP = PAIRED_TILE // GROUP
assert 1 in SPLIT[2] and LOAD_TILES == 2 * GROUP
assert PAIRED_TILE % GROUP == 0 and PAIRED_GROUP not in SPLIT[2] + SPLIT[1]
TURN_ORDER = (0, 2, 1)
TURN_SPLITS = [(layer, g) for layer in TURN_ORDER
               for g in sorted(SPLIT[layer] + (() if layer == 0 else (PAIRED_GROUP,)))]
TURN_PAIRED = [(2, PAIRED_GROUP), (1, PAIRED_GROUP)]
TURN_GROUPS = [s for s in TURN_SPLITS if s not in TURN_PAIRED]
SPLIT_GROUPS = {layer: [g for k, g in TURN_SPLITS if k == layer] for layer in TURN_ORDER}
PLACE = {0: L0_AT, 2: L2_AT, 1: L1_AT}
PART_SLOTS = 4
assert len(TURN_GROUPS) % PART_SLOTS == 0
SPLIT_TILES = {layer: [t for g in SPLIT[layer] for t in range(GROUP * g, GROUP * (g + 1))] + [PAIRED_TILE]
               for layer in (1, 2)}
WHOLE_TILES = {layer: [t for t in range(L12_TILES) if t not in SPLIT_TILES[layer]] for layer in (1, 2)}
L0_SPLIT_TILES = GROUP * len(SPLIT[0])
assert SPLIT[0] == tuple(range(len(SPLIT[0]))) and all(n == RF for n in L0_ROWS[:L0_SPLIT_TILES])
VECTOR_LOWS = [(0, 0), (0, 1), (0, 2), (2, PAIRED_GROUP), (1, PAIRED_GROUP)]
PARTS_AFTER = 1
GATHERS_AFTER = {(2, 5): 1, (2, 9): 1, (1, 3): 1, (1, 7): 8}
assert sum(GATHERS_AFTER.values()) == SLOTS

B_LAYERS, B_TOP1 = 0, 3
B_TOP2 = B_TOP1 + HID1 // P
W_TOP3 = B_TOP2 + HID2 // P
SMALL = W_TOP3 + HID2 // P
SELECT_IN_LOOP = 2
COPY_AFTER = 6
SELECT_AFTER = 1
FIRST_COPY_AFTER = 3
FEED_AFTER, DIRECT_AFTER = 4, 6

LOADS = L12_TILES // LOAD_TILES
STORE_AFTER = LOADS - 2
LOAD_DMAS = [2 + (q == PAIRED_TILE // LOAD_TILES) for q in range(LOADS)]
assert PAIRED_TILE % LOAD_TILES == 0
SHIFTED_LOADS = [(0, 4), (4, L0_TILES)]


def interaction_tower(nc, tables, ids_bases, x_select, w0_upper, w0_lower, w1, w2, small,
                      dense_t, w_top1, w_top2, out):
    ctx = ExitStack()
    with ctx:
        def sb(name, shape, dt=F32):
            return ctx.enter_context(nc.sbuf_tensor(name, shape, dt))

        def bank(name):
            return ctx.enter_context(nc.psum_tensor(name, [P, COLS], F32))

        def sem(name):
            return ctx.enter_context(nc.semaphore(name))

        x_dram = nc.dram_tensor("x_dram", (CHUNKS, STORED_ROWS, COLS), F32, kind="Internal").ap()

        ids_sb = sb("ids_sb", [RF, 2, CHUNKS * SLOTS], I32)
        rows_sb = sb("rows_sb", [RF, CHUNKS * SLOTS], I32)
        x_sel_r = sb("x_sel_r", [RF, REP, RF], F32R)
        w0_sb = sb("w0_sb", [RF, L0_TILES, MAPS])
        w0_hi = sb("w0_hi", [RF, L0_SPLIT_TILES, MAPS], F32R)
        w0_lo = sb("w0_lo", [RF, L0_SPLIT_TILES, MAPS], F32R)
        w1_whole = sb("w1_whole", [P, len(WHOLE_TILES[1]), MAPS])
        w2_whole = sb("w2_whole", [P, len(WHOLE_TILES[2]), MAPS])
        w1_hi = sb("w1_hi", [P, len(SPLIT_TILES[1]), MAPS], F32R)
        w1_lo = sb("w1_lo", [P, len(SPLIT_TILES[1]), MAPS], F32R)
        w2_hi = sb("w2_hi", [P, len(SPLIT_TILES[2]), MAPS], F32R)
        w2_lo = sb("w2_lo", [P, len(SPLIT_TILES[2]), MAPS], F32R)
        small_sb = sb("small_sb", [P, SMALL])
        wt1_sb = sb("wt1_sb", [P, 2, HID1])
        wt1d_sb = sb("wt1d_sb", [DENSE, HID1])
        wt2_sb = sb("wt2_sb", [P, HID1 // P, HID2])
        dense_sb = sb("dense_sb", [DENSE, BATCH])

        rows_now = sb("rows_now", [RF, SLOTS], I32)
        gathered = sb("gathered", [RF, SLOTS * DIM])
        gathered_hi = sb("gathered_hi", [RF, SLOTS * DIM], F32R)
        gathered_lo = sb("gathered_lo", [RF, SLOTS * DIM], F32R)
        x_rows = sb("x_rows", [STORED_ROWS, COLS])
        x_shifted = sb("x_shifted", [RF, L0_TILES, COLS])
        x_spread = sb("x_spread", [P, L12_TILES, COLS])
        products = sb("products", [P, PRODUCT_SLOTS, GROUP, COLS])
        highs = sb("highs", [P, PART_SLOTS, GROUP, COLS], F32R)
        lows = sb("lows", [P, PART_SLOTS, GROUP, COLS], F32R)
        paired = sb("paired", [P, COLS], F32R)
        direct01 = sb("direct01", [P, COLS])
        direct2 = sb("direct2", [P, COLS])
        feats = sb("feats", [P, 2, BATCH])
        y_sb = sb("y_sb", [1, BATCH])

        def room(tile, rows, inner, count):
            tiles = -(-inner * count // COLS)
            return x_spread[0:rows, tile:tile + tiles, :].rearrange("p a n -> p (a n)")[:, 0:inner * count].rearrange(
                "p (j s) -> p j s", s=inner)
        w0l_sb = room(0, RF, MAPS, L0_TILES)
        x_sel = room(2, RF, RF, REP)
        w1_split = room(LOAD_TILES, P, MAPS, len(SPLIT_TILES[1]))
        w2_split = room(2 * LOAD_TILES, P, MAPS, len(SPLIT_TILES[2]))
        hid1 = products[:, 0:2, :, :].rearrange("p a b n -> p (a b) n")
        hid2 = products[:, 2, :, :]

        x_bank = bank("x_bank")
        x1 = bank("x1")
        x2 = bank("x2")
        z0, z1, z2 = bank("z0"), bank("z1"), bank("z2")
        hid1_banks = [bank("hid1_bank0"), bank("hid1_bank1"), x1, x_bank]
        hid2_banks = [z0, z1]
        y_bank = z2

        ids_in = sem("ids_in")
        consts_in = sem("consts_in")
        w0_in = sem("w0_in")
        w_split_in = sem("w_split_in")
        w_whole_in = sem("w_whole_in")
        tower_in = sem("tower_in")
        pool_waits = sem("pool_waits")
        sp_waits = sem("sp_waits")
        rows_known = sem("rows_known")
        w0_ready = sem("w0_ready")
        w0_hi_ready = sem("w0_hi_ready")
        w0_lo_ready = sem("w0_lo_ready")
        w_hi_ready = sem("w_hi_ready")
        w_lo_ready = sem("w_lo_ready")
        x_sel_ready = sem("x_sel_ready")
        rows_copied = sem("rows_copied")
        gathers_done = sem("gathers_done")
        gathered_hi_made = sem("gathered_hi_made")
        gathered_lo_made = sem("gathered_lo_made")
        x_selected = sem("x_selected")
        x_copied = sem("x_copied")
        x_stored = sem("x_stored")
        x_shifted_in = [sem(f"x_shifted_in{k}") for k in range(len(SHIFTED_LOADS))]
        x_spread_in = [sem(f"x_spread_in{q}") for q in range(LOADS)]
        products_made = sem("products_made")
        his_made = sem("his_made")
        pool_lows = sem("pool_lows")
        vector_lows = sem("vector_lows")
        groups_used = sem("groups_used")
        z0_read = sem("z0_read")
        z1_read = sem("z1_read")
        z2_read = sem("z2_read")
        direct01_summed = sem("direct01_summed")
        direct2_summed = sem("direct2_summed")
        tower_mm = sem("tower_mm")
        tower_act = sem("tower_act")
        stored = sem("stored")

        block = ctx.enter_context(nc.Block())

        def group(c, place):
            return GROUPS * (c + 1) - PROLOGUE_AT + place

        def halves(w):
            return slice(0, w.shape[1] // 2), slice(w.shape[1] // 2, w.shape[1])

        def products_of(c, layer, g, at):
            return group(c, at + (1 - g if layer == 2 and g < 2 else g)) + 1

        def skipped(c, mine):
            return sum(k == 0 for k, _ in mine) if isinstance(c, int) and c == CHUNKS - 1 else 0

        def part_made(c, layer, g):
            return (len(TURN_SPLITS) * c + len(SPLIT_GROUPS[1]) + TURN_SPLITS.index((layer, g)) + 1
                    - skipped(c, TURN_SPLITS))

        def low_made(c, layer, g):
            by_vector = (layer, g) in VECTOR_LOWS
            mine = [s for s in TURN_SPLITS if (s in VECTOR_LOWS) == by_vector]
            done = len(mine) * c + sum(k == 1 for k, _ in mine) + mine.index((layer, g)) + 1 - skipped(c, mine)
            return (vector_lows if by_vector else pool_lows), done

        def part_slot(layer, g):
            return TURN_GROUPS.index((layer, g)) % PART_SLOTS

        def slot_freed(c, layer, g):
            mine = TURN_PAIRED if (layer, g) in TURN_PAIRED else TURN_GROUPS
            before = mine.index((layer, g)) - (1 if mine is TURN_PAIRED else PART_SLOTS)
            k, m = mine[before]
            return group(c if before >= 0 else c - 1, PLACE[k] + m) + 1

        def low_part(engine, layer, g, at):
            if (layer, g) in TURN_PAIRED:
                u = products[HALF:P, (at + g) % PRODUCT_SLOTS, PAIRED_TILE % GROUP, :]
                hi = paired[HALF:P, :]
                lo = hi
            else:
                n = RF if layer == 0 else P
                u = products[0:n, (at + g) % PRODUCT_SLOTS, :, :]
                hi = highs[0:n, part_slot(layer, g), :, :]
                lo = lows[0:n, part_slot(layer, g), :, :]
            return engine.tensor_tensor(lo, u, hi.bitcast(F32), ALU.subtract)

        def since(count, semaphore, eng):
            if not isinstance(count, int) or count > 0:
                eng.wait_ge(semaphore, count)

        @block.sync
        def _(sp):
            sp.dma_start(ids_sb[:, :, :], ids_bases).then_inc(ids_in, 16)
            sp.dma_start(x_sel, x_select).then_inc(consts_in, 16)
            sp.dma_start(w0_sb[:, :, :], w0_upper).then_inc(w0_in, 16)
            sp.dma_start(w0l_sb, w0_lower).then_inc(w0_in, 16)
            sp.dma_start(small_sb[:, :], small).then_inc(consts_in, 16)
            for part, w in ((w1_split, w1), (w2_split, w2)):
                sp.dma_start(part, w[:, 0:part.shape[1], :]).then_inc(w_split_in, 16)
            for part, w in ((w1_whole, w1), (w2_whole, w2)):
                sp.dma_start(part[:, :, :], w[:, w.shape[1] - part.shape[1]:, :]).then_inc(w_whole_in, 16)

            def store_x(c):
                sp.wait_ge(x_copied, c + 1)
                sp.dma_start(x_dram[c], x_rows[:, :]).then_inc(x_stored, 16)

            def load_shifted(c, used=0):
                sp.wait_ge(x_stored, 16 * (c + 1))
                sp.sem_inc(sp_waits, 1)
                since(used, products_made, sp)
                for k, (t0, t1) in enumerate(SHIFTED_LOADS):
                    for r in range(REP):
                        tiles = len(range(r + REP * t0, min(SHIFTS, r + REP * t1), REP))
                        src = x_dram[c, r + REP * t0:r + REP * t0 + FIELDS, :]
                        sp.dma_start(
                            x_shifted[r * FIELDS:(r + 1) * FIELDS, t0:t0 + tiles, :],
                            bass.AP(tensor=src.tensor, offset=src.offset,
                                    ap=[[COLS, FIELDS], [REP * COLS, tiles], [1, COLS]])).then_inc(x_shifted_in[k], 16)

            def load_spread(c, q):
                t0, t1 = q * LOAD_TILES, (q + 1) * LOAD_TILES
                if t0 == PAIRED_TILE:
                    sp.dma_start(x_spread[:, t0, :],
                                 x_dram[c, TILE_FIELDS[t0][0], :].partition_broadcast(P)).then_inc(x_spread_in[q], 16)
                    t0 += 1
                for i in range(2):
                    f = TILE_FIELDS[t0][i]
                    sp.dma_start(x_spread[i * HALF:(i + 1) * HALF, t0:t1, :],
                                 x_dram[c, f:f + 2 * (t1 - t0) - 1:2, :].partition_broadcast(HALF)
                                 ).then_inc(x_spread_in[q], 16)

            store_x(0)
            load_shifted(0)
            sp.wait_ge(w0_ready, 1)
            sp.wait_ge(x_sel_ready, 1)
            for q in range(LOADS):
                if q > 0:
                    sp.wait_ge(w_lo_ready, 2 * min(q, 2))
                load_spread(0, q)
            store_x(1)
            load_shifted(1, L0_GROUPS)
            sp.dma_start(wt1_sb[:, :, :], w_top1[0:2 * P, :].rearrange("(a p) m -> p a m", p=P)).then_inc(tower_in, 16)
            sp.dma_start(wt1d_sb[:, :], w_top1[2 * P:2 * P + DENSE, :]).then_inc(tower_in, 16)
            sp.dma_start(wt2_sb[:, :, :], w_top2.rearrange("(a p) m -> p a m", p=P)).then_inc(tower_in, 16)
            sp.dma_start(dense_sb[:, :], dense_t).then_inc(tower_in, 16)

            def turn(c, more):
                for q in range(LOADS):
                    sp.wait_ge(products_made, group(c, L2_AT + (q + 1) * LOAD_TILES // GROUP))
                    load_spread(c + 1, q)
                    if more and q == STORE_AFTER:
                        store_x(c + 2)
                if more:
                    load_shifted(c + 2, group(c, L2_AT))

            with sp.Fori(0, CHUNKS - 2) as c:
                turn(c, True)
            turn(CHUNKS - 2, False)
            sp.wait_ge(tower_act, HID1 // P + HID2 // P + 1)
            sp.dma_start(out, y_sb[:, :]).then_inc(stored, 16)
            sp.wait_ge(stored, 16)

        @block.gpsimd
        def _(pool):
            def wait(semaphore, count):
                pool.wait_ge(semaphore, count)
                pool.sem_inc(pool_waits, 1)

            def take_rows(c):
                nc.gpsimd.tensor_copy(rows_now[:, :], rows_sb[:, bass.ds(c * SLOTS, SLOTS)]).then_inc(rows_copied, 1)
                wait(rows_copied, c + 1)

            def gather(slots):
                for i in slots:
                    nc.gpsimd.indirect_dma_start(
                        out=gathered[:, i * DIM:(i + 1) * DIM], out_offset=None, in_=tables,
                        in_offset=bass.IndirectOffsetOnAxis(ap=rows_now[:, i:i + 1], axis=0),
                    ).then_inc(gathers_done, 16)

            def gathered_low(c):
                since(c, x_selected, pool)
                pool.wait_ge(gathered_hi_made, c + 1)
                nc.gpsimd.tensor_tensor(gathered_lo[:, :], gathered[:, :], gathered_hi[:, :].bitcast(F32),
                                        ALU.subtract).then_inc(gathered_lo_made, 1)

            def low_parts(c, layer, at, select=False, gathers=False):
                for g in SPLIT_GROUPS[layer]:
                    if (layer, g) not in VECTOR_LOWS:
                        pool.wait_ge(his_made, part_made(c, layer, g))
                        low_part(nc.gpsimd, layer, g, at).then_inc(pool_lows, 1)
                    if select and (layer, g) == (2, PARTS_AFTER):
                        gathered_low(c + 2)
                        if gathers:
                            wait(gathered_lo_made, c + 3)
                            take_rows(c + 3)
                    if gathers and (layer, g) in GATHERS_AFTER:
                        places = list(GATHERS_AFTER)
                        before = sum(GATHERS_AFTER[place] for place in places[:places.index((layer, g))])
                        gather(range(before, before + GATHERS_AFTER[layer, g]))

            def turn(c, more, gathers):
                low_parts(c, 2, L2_AT, more, gathers)
                low_parts(c, 1, L1_AT, more, gathers)

            wait(rows_known, 1)
            for c in range(2):
                if c > 0:
                    wait(gathered_lo_made, c)
                take_rows(c)
                gather(range(SLOTS))
                gathered_low(c)
            wait(gathered_lo_made, 2)
            take_rows(2)
            gather(range(SLOTS - sum(n for (layer, g), n in GATHERS_AFTER.items() if layer == 1)))
            low_parts(-1, 1, L1_AT, gathers=True)
            with pool.Fori(0, CHUNKS - 3) as c:
                turn(c, True, True)
            turn(CHUNKS - 3, True, False)
            turn(CHUNKS - 2, False, False)
            low_parts(CHUNKS - 1, 2, 0)

        @block.scalar
        def _(act):
            def copy_x(c):
                act.wait_ge(x_selected, c + 1)
                since(16 * c, x_stored, act)
                nc.scalar.activation(x_rows[:, :], x_bank[0:STORED_ROWS, :], ACT.Copy).then_inc(x_copied, 1)

            def gathered_high(c):
                act.wait_ge(gathers_done, 16 * SLOTS * (c + 1))
                since(c, x_selected, act)
                nc.scalar.activation(gathered_hi[:, :], gathered[:, :], ACT.Copy).then_inc(gathered_hi_made, 1)

            def feed(z, z_made, z_read, x_next, x_used, bias_at):
                act.wait_ge(groups_used, z_made)
                since(x_used, products_made, act)
                bias = small_sb[0:HALF, bias_at:bias_at + 1]
                nc.scalar.activation(x_next[0:HALF, :], z[0:HALF, :], ACT.Relu, bias=bias).then_inc(z_read, 1)
                nc.scalar.activation(x_next[HALF:P, :], z[0:HALF, :], ACT.Relu, bias=bias).then_inc(z_read, 1)

            def layer0_feed(c):
                prologue = isinstance(c, int) and c < 0
                feed(z0, L0_GROUPS if prologue else group(c, L2_AT), z0_read, x1, 0 if prologue else group(c, 0), 0)

            def layer0_direct(c):
                since(c + 1, direct01_summed, act)
                nc.scalar.activation(direct01[0:HALF, :], z0[HALF:P, :], ACT.Relu,
                                     bias=small_sb[HALF:P, 0:1]).then_inc(z0_read, 1)

            def layer1_out(c):
                feed(z1, group(c, 0), z1_read, x2, group(c - 1, L1_AT), 1)
                nc.scalar.activation(direct01[HALF:P, :], z1[HALF:P, :], ACT.Relu,
                                     bias=small_sb[HALF:P, 1:2]).then_inc(z1_read, 1)

            def layer2_out(c, at=L2_AT):
                act.wait_ge(groups_used, group(c, at + L12_GROUPS))
                act.wait_ge(direct2_summed, c + 1)
                nc.scalar.activation(direct2[:, :], z2[:, :], ACT.Relu, bias=small_sb[:, 2:3]).then_inc(z2_read, 1)

            def high_part(c, layer, g, at):
                act.wait_ge(products_made, products_of(c, layer, g, at))
                since(slot_freed(c, layer, g), groups_used, act)
                slot = (at + g) % PRODUCT_SLOTS
                if (layer, g) in TURN_PAIRED:
                    src, dst = products[:, slot, PAIRED_TILE % GROUP, :], paired[:, :]
                else:
                    n = RF if layer == 0 else P
                    src, dst = products[0:n, slot, :, :], highs[0:n, part_slot(layer, g), :, :]
                nc.scalar.activation(dst, src, ACT.Copy).then_inc(his_made, 1)

            act.sem_inc(z2_read, 1)
            act.wait_ge(consts_in, 2 * 16)
            nc.scalar.activation(y_sb[0:1, 0:1], small_sb[0:1, 0:1], ACT.Relu)
            nc.scalar.activation(x_sel_r[:, :, :], x_sel, ACT.Copy).then_inc(x_sel_ready, 1)
            act.wait_ge(w0_ready, 1)
            nc.scalar.activation(w0_hi[:, :, :], w0_sb[:, 0:L0_SPLIT_TILES, :], ACT.Copy).then_inc(w0_hi_ready, 1)
            act.wait_ge(w_split_in, 2 * 16)
            for w, w_hi in ((w1_split, w1_hi), (w2_split, w2_hi)):
                for tiles in halves(w):
                    nc.scalar.activation(w_hi[:, tiles, :], w[:, tiles, :], ACT.Copy).then_inc(w_hi_ready, 1)
            gathered_high(0)
            copy_x(0)
            gathered_high(1)
            layer0_feed(-1)
            layer0_direct(-1)
            for g in SPLIT_GROUPS[1]:
                high_part(-1, 1, g, L1_AT)
                if g == FIRST_COPY_AFTER:
                    copy_x(1)

            def turn(c, more):
                for g in SPLIT_GROUPS[0]:
                    high_part(c, 0, g, L0_AT)
                layer1_out(c)
                for g in range(L12_GROUPS):
                    if g in SPLIT_GROUPS[2]:
                        high_part(c, 2, g, L2_AT)
                    if more and g == PARTS_AFTER:
                        gathered_high(c + 2)
                    if g == FEED_AFTER:
                        layer0_feed(c)
                    if g == DIRECT_AFTER:
                        layer0_direct(c)
                    if more and g == COPY_AFTER:
                        copy_x(c + 2)
                for g in SPLIT_GROUPS[1]:
                    high_part(c, 1, g, L1_AT)
                layer2_out(c)

            with act.Fori(0, CHUNKS - 2) as c:
                turn(c, True)
            turn(CHUNKS - 2, False)
            layer1_out(CHUNKS - 1)
            for g in SPLIT_GROUPS[2]:
                high_part(CHUNKS - 1, 2, g, 0)
            layer2_out(CHUNKS - 1, 0)

            act.wait_ge(tower_in, 4 * 16)
            for m in range(HID1 // P):
                act.wait_ge(tower_mm, m + 1)
                nc.scalar.activation(hid1[:, m, :], hid1_banks[m][:, :], ACT.Relu,
                                     bias=small_sb[:, B_TOP1 + m:B_TOP1 + m + 1]).then_inc(tower_act, 1)
            for m in range(HID2 // P):
                act.wait_ge(tower_mm, HID1 // P + m + 1)
                nc.scalar.activation(hid2[:, m, :], hid2_banks[m][:, :], ACT.Relu,
                                     bias=small_sb[:, B_TOP2 + m:B_TOP2 + m + 1]).then_inc(tower_act, 1)
            act.wait_ge(tower_mm, HID1 // P + HID2 // P + 1)
            nc.scalar.activation(y_sb[:, :], y_bank[0:1, :], ACT.Copy).then_inc(tower_act, 1)

        @block.vector
        def _(dve):
            dve.sem_inc(direct2_summed, 1)
            dve.wait_ge(ids_in, 16)
            nc.vector.tensor_tensor(rows_sb[:, :], ids_sb[:, 0, :], ids_sb[:, 1, :], ALU.add).then_inc(rows_known, 1)
            dve.wait_ge(w0_in, 2 * 16)
            nc.vector.tensor_tensor(w0_sb[:, :, :], w0_sb[:, :, :], w0l_sb, ALU.add).then_inc(w0_ready, 1)
            dve.wait_ge(w0_hi_ready, 1)
            nc.vector.tensor_tensor(w0_lo[:, :, :], w0_sb[:, 0:L0_SPLIT_TILES, :],
                                    w0_hi[:, :, :].bitcast(F32), ALU.subtract).then_inc(w0_lo_ready, 1)
            for k, (w, w_hi, w_lo) in enumerate(((w1_split, w1_hi, w1_lo), (w2_split, w2_hi, w2_lo))):
                for i, tiles in enumerate(halves(w)):
                    dve.wait_ge(w_hi_ready, 2 * k + i + 1)
                    nc.vector.tensor_tensor(w_lo[:, tiles, :], w[:, tiles, :],
                                            w_hi[:, tiles, :].bitcast(F32), ALU.subtract).then_inc(w_lo_ready, 1)

            def multiply(c, place, groups, tiles, spread, x):
                since(group(c, place) - PRODUCT_SLOTS + groups, groups_used, dve)
                n = spread.shape[0]
                slot = place % PRODUCT_SLOTS
                made = products[0:n, slot:slot + groups, :, :].rearrange("p g t n -> p (g t) n")[:, 0:tiles, :]
                nc.vector.tensor_tensor(made, spread, x[0:n, :].unsqueeze(1).to_broadcast([n, tiles, COLS]),
                                        ALU.mult).then_inc(products_made, groups)

            def layer0_products(c, at=L0_AT):
                dve.wait_ge(x_selected, c + 2)
                for k, (first, end) in enumerate(SHIFTED_LOADS):
                    dve.wait_ge(x_shifted_in[k], 16 * REP * (c + 2))
                    t0 = first
                    while t0 < end:
                        t1 = t0
                        while t1 < end and L0_ROWS[t1] == L0_ROWS[t0]:
                            t1 += 1
                        multiply(c, at + t0 // GROUP, -(-(t1 - t0) // GROUP), t1 - t0,
                                 x_shifted[0:L0_ROWS[t0], t0:t1, :], x_bank)
                        t0 = t1

            later = []

            def low_parts():
                for c, layer, g, at in later:
                    dve.wait_ge(his_made, part_made(c, layer, g))
                    low_part(nc.vector, layer, g, at).then_inc(vector_lows, 1)
                later.clear()

            def layer_products(c, layer, at, x, loaded, sums):
                for q in range(LOADS):
                    if loaded is not None:
                        dve.wait_ge(x_spread_in[q], LOAD_DMAS[q] * 16 * loaded)
                    g = q * LOAD_TILES // GROUP
                    if layer == 2 and q == 0:
                        for m in (1, 0):
                            multiply(c, at + m, 1, GROUP, x_spread[:, m * GROUP:(m + 1) * GROUP, :], x)
                    else:
                        multiply(c, at + g, LOAD_TILES // GROUP, LOAD_TILES,
                                 x_spread[:, q * LOAD_TILES:(q + 1) * LOAD_TILES, :], x)
                    low_parts()
                    later.extend((c, layer, m, at) for m in range(g, g + LOAD_TILES // GROUP)
                                 if (layer, m) in VECTOR_LOWS)
                    if q in sums:
                        sums[q]()

            def layer1_products(c, sums):
                dve.wait_ge(z0_read, 3 * (c + 1) + 2)
                layer_products(c, 1, L1_AT, x1, c + 2, sums)

            def layer2_products(c, sums, at=L2_AT):
                dve.wait_ge(z1_read, 3 * c + 2)
                layer_products(c, 2, at, x2, None, sums)

            def sum_direct(direct, half, c, summed):
                nc.vector.tensor_reduce(
                    feats[:, half, bass.ds(c * CHUNK_ROWS, CHUNK_ROWS)],
                    direct[:, :].rearrange("p (b d) -> p b d", d=DIM), AX_X, ALU.add).then_inc(summed, 1)

            def sum01(c):
                dve.wait_ge(z1_read, 3 * c + 3)
                dve.wait_ge(z0_read, 3 * c + 3)
                sum_direct(direct01, 0, c, direct01_summed)

            def sum2(c):
                dve.wait_ge(z2_read, c + 2)
                sum_direct(direct2, 1, c, direct2_summed)

            layer0_products(-1, PROLOGUE_AT)
            layer1_products(-1, {})
            with dve.Fori(0, CHUNKS - 1) as c:
                layer0_products(c)
                later.extend((c, 0, g, L0_AT) for g in SPLIT[0])
                low_parts()
                layer2_products(c, {3: lambda: sum01(c)})
                layer1_products(c, {LOADS - 1: lambda: sum2(c)})
            assert not later
            layer2_products(CHUNKS - 1, {1: lambda: sum01(CHUNKS - 1)}, 0)
            low_parts()
            sum2(CHUNKS - 1)

        @block.tensor
        def _(pe):
            def select_x(c, made=None):
                pe.wait_ge(gathered_lo_made, c + 1)
                since(c, x_copied, pe)
                if made is not None:
                    pe.wait_ge(products_made, made)
                cols = x_bank[0:RF, :].rearrange("p (b d) -> p b d", d=DIM)
                for r in range(REP):
                    k = len(range(r, CHUNK_ROWS, REP))
                    for part in (gathered_hi, gathered_lo):
                        last = nc.tensor.matmul(
                            cols[:, r:r + REP * (k - 1) + 1:REP, :], x_sel_r[:, r, :],
                            part[:, 0:k * DIM].rearrange("p (i d) -> p i d", d=DIM),
                            start=(part is gathered_hi), stop=(part is gathered_lo))
                last.then_inc(x_selected, 1)

            def layer0(c, at=L0_AT, split=True):
                for g in range(L0_GROUPS):
                    if split and g in SPLIT[0]:
                        pe.wait_ge(*low_made(c, 0, g))
                        for i in range(GROUP):
                            t = g * GROUP + i
                            hi = highs[0:RF, part_slot(0, g), i, :]
                            lo = lows[0:RF, part_slot(0, g), i, :]
                            for w, part in ((w0_hi, hi), (w0_lo, hi), (w0_hi, lo)):
                                last = nc.tensor.matmul(z0[:, :], w[:, t, :], part,
                                                        start=(t == 0 and w is w0_hi and part is hi), stop=False)
                        last.then_inc(groups_used, 1)
                        continue
                    pe.wait_ge(products_made, group(c, at + g) + 1)
                    for t in range(g * GROUP, min((g + 1) * GROUP, L0_TILES)):
                        n = L0_ROWS[t]
                        last = nc.tensor.matmul(z0[:, :], w0_sb[0:n, t, :],
                                                products[0:n, (at + g) % PRODUCT_SLOTS, t % GROUP, :],
                                                start=(t == 0), stop=(t == L0_TILES - 1))
                    last.then_inc(groups_used, 1)

            def layer(c, layer, at, z, w_whole, w_hi, w_lo, between):
                def add(weights, moving, first=False, last=False):
                    return nc.tensor.matmul(z[:, :], weights, moving, start=first, stop=last)

                for g in range(L12_GROUPS):
                    slot = (at + g) % PRODUCT_SLOTS
                    if g in SPLIT[layer]:
                        pe.wait_ge(*low_made(c, layer, g))
                    else:
                        pe.wait_ge(products_made, products_of(c, layer, g, at))
                    for t in reversed(range(g * GROUP, (g + 1) * GROUP)):
                        ends = dict(first=(t == GROUP - 1), last=(t == L12_TILES - GROUP))
                        if t == PAIRED_TILE:
                            pe.wait_ge(*low_made(c, layer, g))
                            k = SPLIT_TILES[layer].index(t)
                            add(w_lo[0:HALF, k, :], paired[0:HALF, :])
                            last = add(w_hi[:, k, :], paired[:, :])
                        elif g in SPLIT[layer]:
                            k = SPLIT_TILES[layer].index(t)
                            hi = highs[:, part_slot(layer, g), t % GROUP, :]
                            lo = lows[:, part_slot(layer, g), t % GROUP, :]
                            add(w_hi[:, k, :], hi, first=ends["first"])
                            add(w_lo[:, k, :], hi)
                            last = add(w_hi[:, k, :], lo, last=ends["last"])
                        else:
                            last = add(w_whole[:, WHOLE_TILES[layer].index(t), :],
                                       products[:, slot, t % GROUP, :], **ends)
                    last.then_inc(groups_used, 1)
                    if g in between:
                        between[g]()

            def layer1(c, between={}):
                layer(c, 1, L1_AT, z1, w1_whole, w1_hi, w1_lo, between)

            def layer2(c, at=L2_AT, between={}):
                layer(c, 2, at, z2, w2_whole, w2_hi, w2_lo, between)

            pe.wait_ge(x_sel_ready, 1)
            select_x(0)
            pe.wait_ge(w0_ready, 1)
            layer0(-1, PROLOGUE_AT, False)
            pe.wait_ge(w_whole_in, 2 * 16)
            pe.wait_ge(w_lo_ready, 2 * 2)
            pe.wait_ge(w0_lo_ready, 1)
            layer1(-1, {SELECT_AFTER: lambda: select_x(1, L0_GROUPS)})

            def turn(c, more):
                pe.wait_ge(z0_read, 3 * (c + 1))
                layer0(c)
                pe.wait_ge(z2_read, c + 1)
                layer2(c, between={SELECT_IN_LOOP: lambda: select_x(c + 2, group(c, L2_AT))} if more else {})
                pe.wait_ge(z1_read, 3 * (c + 1))
                layer1(c)

            with pe.Fori(0, CHUNKS - 2) as c:
                turn(c, True)
            turn(CHUNKS - 2, False)
            pe.wait_ge(tower_in, 4 * 16)
            for m in range(2):
                nc.tensor.matmul(hid1_banks[m][:, :], wt1d_sb[:, m * P:(m + 1) * P], dense_sb[:, :],
                                 start=True, stop=False)
            pe.wait_ge(z2_read, CHUNKS)
            layer2(CHUNKS - 1, 0)
            pe.wait_ge(direct01_summed, CHUNKS)
            pe.wait_ge(z0_read, 3 * CHUNKS)
            pe.wait_ge(z1_read, 3 * CHUNKS)
            for m in range(HID1 // P):
                cols = slice(m * P, (m + 1) * P)
                if m >= 2:
                    nc.tensor.matmul(hid1_banks[m][:, :], wt1d_sb[:, cols], dense_sb[:, :], start=True, stop=False)
                nc.tensor.matmul(hid1_banks[m][:, :], wt1_sb[:, 0, cols], feats[:, 0, :], start=False, stop=False)
            pe.wait_ge(z2_read, CHUNKS + 1)
            pe.wait_ge(direct2_summed, CHUNKS + 1)
            for m in range(HID1 // P):
                cols = slice(m * P, (m + 1) * P)
                nc.tensor.matmul(hid1_banks[m][:, :], wt1_sb[:, 1, cols], feats[:, 1, :],
                                 start=False, stop=True).then_inc(tower_mm, 1)
            for a in range(HID1 // P):
                pe.wait_ge(tower_act, a + 1)
                for m in range(HID2 // P):
                    mm = nc.tensor.matmul(hid2_banks[m][:, :], wt2_sb[:, a, m * P:(m + 1) * P],
                                          hid1[:, a, :], start=(a == 0), stop=(a == HID1 // P - 1))
                    if a == HID1 // P - 1:
                        mm.then_inc(tower_mm, 1)
            for m in range(HID2 // P):
                pe.wait_ge(tower_act, HID1 // P + m + 1)
                mm = nc.tensor.matmul(y_bank[0:1, :], small_sb[:, W_TOP3 + m:W_TOP3 + m + 1], hid2[:, m, :],
                                      start=(m == 0), stop=(m == HID2 // P - 1))
            mm.then_inc(tower_mm, 1)


def kernel(**inputs):
    import concourse.bacc as bacc
    from concourse.bass_utils import run_bass_kernel_spmd

    def arr(name):
        return np.ascontiguousarray(inputs[name])

    tables = [arr(f"tbl_{f}") for f in range(FIELDS)]
    starts = np.cumsum([0] + [t.shape[0] for t in tables[:-1]]).astype(np.int32)
    ids = arr("ids").astype(np.int32)

    padded = np.zeros((CHUNKS, SLOTS * REP, FIELDS), np.int32)
    padded[:, :CHUNK_ROWS] = ids.reshape(CHUNKS, CHUNK_ROWS, FIELDS)
    ids_laid = padded.reshape(CHUNKS, SLOTS, REP, FIELDS).transpose(2, 3, 0, 1).reshape(RF, CHUNKS * SLOTS)
    bases = np.tile(starts, REP)[:, None] + np.zeros((RF, CHUNKS * SLOTS), np.int32)

    f = np.arange(FIELDS)
    x_select = np.zeros((RF, REP, RF), np.float32)
    for r in range(REP):
        for q in range(REP):
            x_select[r * FIELDS + f, r, q * FIELDS + f] = 1

    w0 = arr("L0_rec_w0")
    upper = np.zeros((L0_TILES * REP, FIELDS, MAPS), np.float32)
    lower = np.zeros_like(upper)
    for s in range(SHIFTS):
        upper[s] = w0[f, (f + s) % FIELDS]
        if s:
            lower[s] = w0[(f + s) % FIELDS, f]

    def tiled(w):
        return np.ascontiguousarray(w.reshape(L0_TILES, RF, MAPS).transpose(1, 0, 2))

    def split_first(w, layer):
        halves = w.reshape(FIELDS, HALF, MAPS)[np.array(TILE_FIELDS)]
        order = SPLIT_TILES[layer] + WHOLE_TILES[layer]
        return np.ascontiguousarray(halves.reshape(L12_TILES, P, MAPS)[order].transpose(1, 0, 2))

    def column(name, parts):
        return np.ascontiguousarray(arr(name).reshape(parts, P).T)

    feeds = {
        "tables": np.concatenate(tables, axis=0),
        "ids_bases": np.ascontiguousarray(np.stack([ids_laid, bases], axis=1)),
        "x_select": x_select,
        "w0_upper": tiled(upper),
        "w0_lower": tiled(lower),
        "w1": split_first(arr("L0_rec_w1"), 1),
        "w2": split_first(arr("L0_rec_w2"), 2),
        "small": np.ascontiguousarray(np.concatenate([
            column("L0_rec_b0", 1), column("L0_rec_b1", 1), column("L0_rec_b2", 1),
            column("b_top1", HID1 // P), column("b_top2", HID2 // P), column("W_top3", HID2 // P)], axis=1)),
        "dense_t": np.ascontiguousarray(arr("dense_ctx").T),
        "w_top1": arr("W_top1"),
        "w_top2": arr("W_top2"),
    }
    nc = bacc.Bacc("TRN2", target_bir_lowering=False, num_devices=1)
    args = [nc.dram_tensor(f"in_{k}", a.shape, mybir.dt.from_np(a.dtype), kind="ExternalInput").ap()
            for k, a in feeds.items()]
    args.append(nc.dram_tensor("out_y", (1, BATCH), F32, kind="ExternalOutput").ap())
    interaction_tower(nc, *args)
    r = run_bass_kernel_spmd(nc, [{f"in_{k}": a for k, a in feeds.items()}], core_ids=[0])
    return r.results[0]["out_y"].reshape(BATCH, 1)
```
